# Optimizing a Trainium2 kernel written in Bass

```python
import numpy as np
import jax
import jax.numpy as jnp

def _softmax(x, axis=-1):
    return jax.nn.softmax(x, axis=axis)

def _gelu(x):
    return jax.nn.gelu(x, approximate=True)

def _silu(x):
    return jax.nn.silu(x)

def _sigmoid(x):
    return jax.nn.sigmoid(x)

def _layernorm(x, axis=-1, eps=1e-05):
    m = jnp.mean(x, axis=axis, keepdims=True)
    v = jnp.var(x, axis=axis, keepdims=True)
    return (x - m) / jnp.sqrt(v + eps)

def _scatter_add(tgt, idx, src, axis=0):
    return tgt.at[idx].add(src)

def _segment_sum(src, seg, n):
    return jax.ops.segment_sum(src, seg, n)
kernel_name = 'mk_gnn_resnorm_d2_gnn_r8_0943e0'

def setup_inputs(seed: int=0):
    np.random.seed(seed)
    _w = jnp.asarray

    def _rec_inputs():
        import jax
        import jax.numpy as jnp
        _gk = jax.random.key(seed)
        x = -0.000202 + 1 * jax.random.normal(jax.random.fold_in(_gk, 1), (12500, 64), jnp.float32)
        src = jax.random.randint(jax.random.fold_in(_gk, 2), (200000,), 0, 12500, jnp.int32)
        dst = jax.random.randint(jax.random.fold_in(_gk, 3), (200000,), 0, 12500, jnp.int32)
        _o = jnp.argsort(dst, stable=True)
        src = src[_o]
        dst = dst[_o]
        edge_attr_32 = 0.000155561 + 1.00019 * jax.random.normal(jax.random.fold_in(_gk, 12), (200000, 32), jnp.float32)
        return (x, src, dst, edge_attr_32)
    x, src, dst, edge_attr_32 = _rec_inputs()

    def _L0_gnn_setup():
        import jax, jax.numpy as jnp
        import numpy as np
        N_NODES = 12500
        N_EDGES = 150000
        N_FEAT = 64
        N_EDGE_FEAT = 32
        HIDDENS = 128
        N_TARGETS = 64

        def _glorot(key, fan_in, fan_out):
            lim = 1.0 / np.sqrt(fan_in)
            return jax.random.uniform(key, (fan_in, fan_out), jnp.float32, -lim, lim)

        def _mlp(h, W1, b1, W2, b2):
            h = jax.nn.leaky_relu(h @ W1 + b1, negative_slope=0.01)
            return h @ W2 + b2
        key = jax.random.key(seed)
        ks = jax.random.split(key, 20)
        inp = {'x': jax.random.normal(ks[0], (N_NODES, N_FEAT), jnp.float32), 'edge_index': jax.random.randint(ks[1], (2, N_EDGES), 0, N_NODES, jnp.int32), 'edge_attr': jax.random.normal(ks[2], (N_EDGES, N_EDGE_FEAT), jnp.float32), 'u': jax.random.normal(ks[3], (1,), jnp.float32), 'batch': jnp.zeros((N_NODES,), jnp.int32)}
        din = N_FEAT + N_EDGE_FEAT
        inp['W1f'] = _glorot(ks[4], din, HIDDENS)
        inp['b1f'] = jnp.zeros((HIDDENS,), jnp.float32)
        inp['W2f'] = _glorot(ks[5], HIDDENS, N_TARGETS)
        inp['b2f'] = jnp.zeros((N_TARGETS,), jnp.float32)
        inp['W1p'] = _glorot(ks[6], din, HIDDENS)
        inp['b1p'] = jnp.zeros((HIDDENS,), jnp.float32)
        inp['W2p'] = _glorot(ks[7], HIDDENS, N_TARGETS)
        inp['b2p'] = jnp.zeros((N_TARGETS,), jnp.float32)
        inp['Wc1'] = _glorot(ks[8], 2 * N_TARGETS, HIDDENS)
        inp['bc1'] = jnp.zeros((HIDDENS,), jnp.float32)
        inp['Wc2'] = _glorot(ks[9], HIDDENS, N_TARGETS)
        inp['bc2'] = jnp.zeros((N_TARGETS,), jnp.float32)
        return inp
    _L0_gnn_all = _L0_gnn_setup()
    _L0_gnn_in = {k: v for k, v in _L0_gnn_all.items() if k in ('u', 'W1f', 'b1f', 'W2f', 'b2f', 'W1p', 'b1p', 'W2p', 'b2p', 'Wc1', 'bc1', 'Wc2', 'bc2')}
    del _L0_gnn_all

    def _L1_gnn_setup():
        import jax, jax.numpy as jnp
        import numpy as np
        N_NODES = 12500
        N_EDGES = 200000
        IN_DIM = 64
        HID = 64
        EPS = 1e-12

        def _sage_layer(x, src, dst, deg_inv, Wl, bl, Wr):
            n = x.shape[0]
            agg = jax.ops.segment_sum(x[src], dst, num_segments=n) * deg_inv
            h = agg @ Wl.T + bl + x @ Wr.T
            norm = jnp.maximum(jnp.linalg.norm(h, axis=-1, keepdims=True), EPS)
            return jax.nn.relu(h / norm)
        key = jax.random.key(seed)
        ks = jax.random.split(key, 8)
        x = jax.random.normal(ks[0], (N_NODES, IN_DIM), dtype=jnp.float32)
        edge_index = jax.random.randint(ks[1], (2, N_EDGES), 0, N_NODES, dtype=jnp.int64)
        s = 1.0 / np.sqrt(IN_DIM)
        Wl0 = jax.random.uniform(ks[2], (HID, IN_DIM), jnp.float32, -s, s)
        bl0 = jnp.zeros((HID,), jnp.float32)
        Wr0 = jax.random.uniform(ks[3], (HID, IN_DIM), jnp.float32, -s, s)
        sh = 1.0 / np.sqrt(HID)
        Wl1 = jax.random.uniform(ks[4], (HID, HID), jnp.float32, -sh, sh)
        bl1 = jnp.zeros((HID,), jnp.float32)
        Wr1 = jax.random.uniform(ks[5], (HID, HID), jnp.float32, -sh, sh)
        return {'x': x, 'edge_index': edge_index, 'Wl0': Wl0, 'bl0': bl0, 'Wr0': Wr0, 'Wl1': Wl1, 'bl1': bl1, 'Wr1': Wr1}
    _L1_gnn_all = _L1_gnn_setup()
    _L1_gnn_in = {k: v for k, v in _L1_gnn_all.items() if k in ('Wl0', 'bl0', 'Wr0', 'Wl1', 'bl1', 'Wr1')}
    del _L1_gnn_all
    return {'x': x, 'src': src, 'dst': dst, 'edge_attr_32': edge_attr_32, 'L0_gnn_u': _L0_gnn_in['u'], 'L0_gnn_W1f': _L0_gnn_in['W1f'], 'L0_gnn_b1f': _L0_gnn_in['b1f'], 'L0_gnn_W2f': _L0_gnn_in['W2f'], 'L0_gnn_b2f': _L0_gnn_in['b2f'], 'L0_gnn_W1p': _L0_gnn_in['W1p'], 'L0_gnn_b1p': _L0_gnn_in['b1p'], 'L0_gnn_W2p': _L0_gnn_in['W2p'], 'L0_gnn_b2p': _L0_gnn_in['b2p'], 'L0_gnn_Wc1': _L0_gnn_in['Wc1'], 'L0_gnn_bc1': _L0_gnn_in['bc1'], 'L0_gnn_Wc2': _L0_gnn_in['Wc2'], 'L0_gnn_bc2': _L0_gnn_in['bc2'], 'L1_gnn_Wl0': _L1_gnn_in['Wl0'], 'L1_gnn_bl0': _L1_gnn_in['bl0'], 'L1_gnn_Wr0': _L1_gnn_in['Wr0'], 'L1_gnn_Wl1': _L1_gnn_in['Wl1'], 'L1_gnn_bl1': _L1_gnn_in['bl1'], 'L1_gnn_Wr1': _L1_gnn_in['Wr1']}

def reference(x, src, dst, edge_attr_32, L0_gnn_u, L0_gnn_W1f, L0_gnn_b1f, L0_gnn_W2f, L0_gnn_b2f, L0_gnn_W1p, L0_gnn_b1p, L0_gnn_W2p, L0_gnn_b2p, L0_gnn_Wc1, L0_gnn_bc1, L0_gnn_Wc2, L0_gnn_bc2, L1_gnn_Wl0, L1_gnn_bl0, L1_gnn_Wr0, L1_gnn_Wl1, L1_gnn_bl1, L1_gnn_Wr1):
    import jax
    import jax.numpy as jnp

    def _L0_gnn_ref(x, edge_index, edge_attr, u, batch, W1f, b1f, W2f, b2f, W1p, b1p, W2p, b2p, Wc1, bc1, Wc2, bc2):
        import jax, jax.numpy as jnp
        import numpy as np
        N_NODES = 12500
        N_EDGES = 150000
        N_FEAT = 64
        N_EDGE_FEAT = 32
        HIDDENS = 128
        N_TARGETS = 64

        def _glorot(key, fan_in, fan_out):
            lim = 1.0 / np.sqrt(fan_in)
            return jax.random.uniform(key, (fan_in, fan_out), jnp.float32, -lim, lim)

        def _mlp(h, W1, b1, W2, b2):
            h = jax.nn.leaky_relu(h @ W1 + b1, negative_slope=0.01)
            return h @ W2 + b2
        n_nodes = x.shape[0]
        n1, n2 = (edge_index[0], edge_index[1])
        future_in = jnp.concatenate([x[n2], edge_attr], axis=1)
        future_out = _mlp(future_in, W1f, b1f, W2f, b2f)
        future_agg = jax.ops.segment_sum(future_out, n1, num_segments=n_nodes)
        past_in = jnp.concatenate([x[n1], edge_attr], axis=1)
        past_out = _mlp(past_in, W1p, b1p, W2p, b2p)
        past_sum = jax.ops.segment_sum(past_out, n2, num_segments=n_nodes)
        counts = jax.ops.segment_sum(jnp.ones((past_out.shape[0],), x.dtype), n2, num_segments=n_nodes)
        past_agg = past_sum / jnp.maximum(counts, 1.0)[:, None]
        flow = jnp.concatenate([past_agg, future_agg], axis=1)
        out = _mlp(flow, Wc1, bc1, Wc2, bc2)
        return out + x

    def _L1_gnn_ref(x, edge_index, Wl0, bl0, Wr0, Wl1, bl1, Wr1):
        import jax, jax.numpy as jnp
        import numpy as np
        N_NODES = 12500
        N_EDGES = 200000
        IN_DIM = 64
        HID = 64
        EPS = 1e-12

        def _sage_layer(x, src, dst, deg_inv, Wl, bl, Wr):
            n = x.shape[0]
            agg = jax.ops.segment_sum(x[src], dst, num_segments=n) * deg_inv
            h = agg @ Wl.T + bl + x @ Wr.T
            norm = jnp.maximum(jnp.linalg.norm(h, axis=-1, keepdims=True), EPS)
            return jax.nn.relu(h / norm)
        src, dst = (edge_index[0], edge_index[1])
        deg = jax.ops.segment_sum(jnp.ones((src.shape[0],), x.dtype), dst, num_segments=x.shape[0])
        deg_inv = (1.0 / jnp.maximum(deg, 1.0))[:, None]
        h = _sage_layer(x, src, dst, deg_inv, Wl0, bl0, Wr0)
        h = _sage_layer(h, src, dst, deg_inv, Wl1, bl1, Wr1)
        return h
    edge_index = jnp.stack([src, dst])
    batch0 = jnp.zeros((12500,), jnp.int32)
    x = _layernorm(x + _L0_gnn_ref(x, edge_index, edge_attr_32, L0_gnn_u, batch0, L0_gnn_W1f, L0_gnn_b1f, L0_gnn_W2f, L0_gnn_b2f, L0_gnn_W1p, L0_gnn_b1p, L0_gnn_W2p, L0_gnn_b2p, L0_gnn_Wc1, L0_gnn_bc1, L0_gnn_Wc2, L0_gnn_bc2), axis=-1)
    x = _layernorm(x + _L1_gnn_ref(x, edge_index, L1_gnn_Wl0, L1_gnn_bl0, L1_gnn_Wr0, L1_gnn_Wl1, L1_gnn_bl1, L1_gnn_Wr1), axis=-1)
    return x

_drawn_inputs = setup_inputs


def setup_inputs(seed=0):
    import zlib

    import numpy as np

    out = dict(_drawn_inputs(seed))
    spreads = {'L0_gnn_b1f': (0.0, 0.1),
     'L0_gnn_b2f': (0.0, 0.1),
     'L0_gnn_b1p': (0.0, 0.8),
     'L0_gnn_b2p': (0.0, 0.8),
     'L0_gnn_bc1': (0.0, 0.358),
     'L0_gnn_bc2': (0.0, 0.1),
     'L1_gnn_bl0': (0.0, 0.8),
     'L1_gnn_bl1': (0.0, 0.1)}
    factors = {'L0_gnn_W1p': 8.0, 'L0_gnn_W2p': 3.815, 'L1_gnn_Wl0': 4.344}
    for name, (base, spread) in spreads.items():
        noise = np.random.default_rng([zlib.crc32(name.encode()), seed]).standard_normal(out[name].shape)
        drawn = base * np.exp(spread * noise) if base else spread * noise
        out[name] = jnp.asarray(drawn.astype(out[name].dtype))
    for name, factor in factors.items():
        out[name] = (out[name] * factor).astype(out[name].dtype)
    return out
```

```python
from contextlib import ExitStack

import concourse.bass as bass
from concourse import mybir

F32 = mybir.dt.float32
I32 = mybir.dt.int32
ALU = mybir.AluOpType
ACT = mybir.ActivationFunctionType
AX_X = mybir.AxisListType.X

P = 128
N = 12500
E = 200000
D = 64
DE = 32
H = 128
TILES = 4
GROUP = TILES * P
GROUPS = -(-E // GROUP)
LAST = E - GROUP
OVERLAP = (GROUPS - 1) * GROUP - LAST
PAIRS = (GROUPS - 1) // 2
W = 64
NW = N + W
CH = 500
CP, CQ = 125, 4
CHUNKS = N // CH
ROWS = 12800
ZCOLS = ROWS * D // P
LOADS = [98, 98, 98, GROUPS - 3 * 98]
EPS_LN = 1e-5
EPS_NORM = 1e-12
SLOPE = 0.01


def build(nc, x, src, dst, ea, W1f, b1f, W2f, b2f, W1p, b1p, W2p, b2p, Wc1, bc1, Wc2, bc2,
          Wl0, bl0, Wr0, Wl1, bl1, Wr1, out):
    Ap = nc.dram_tensor("Ap", [N, H], F32).ap()
    Af = nc.dram_tensor("Af", [NW, H], F32).ap()
    future = [nc.dram_tensor(f"future{q}", [ROWS, D], F32).ap() for q in range(TILES)]
    x1T = nc.dram_tensor("x1T", [CHUNKS, D, CH], F32).ap()
    h1T = nc.dram_tensor("h1T", [CHUNKS, D, CH], F32).ap()
    x1 = nc.dram_tensor("x1", [N, D], F32).ap()
    h1 = nc.dram_tensor("h1", [N, D], F32).ap()

    ctx = ExitStack()
    with ctx:
        def sb(name, shape, dt=F32):
            return ctx.enter_context(nc.sbuf_tensor(name, shape, dt))

        stage = [ExitStack()]

        def tmp(name, shape, dt=F32):
            return stage[0].enter_context(nc.sbuf_tensor(name, shape, dt))

        def next_stage():
            stage[0].close()
            stage[0] = ExitStack()

        def ps(name, shape):
            return ctx.enter_context(nc.psum_tensor(name, shape, F32))

        def sem(name):
            return ctx.enter_context(nc.semaphore(name))

        bank = [ps(f"bank{i}", [P, 512]) for i in range(8)]

        acc = sb("acc", [P, NW])
        cnt = sb("cnt", [D, NW])

        ident = sb("ident", [P, P])
        ident2 = sb("ident2", [P, P])
        triu = sb("triu", [P, P])
        ones = sb("ones", [P, D])
        mean = sb("mean", [D, D])
        window = sb("window", [P, W])
        window_i = sb("window_i", [P, W], I32)
        dump = sb("dump", [P, 1])
        dump_i = sb("dump_i", [P, 1], I32)
        eps = sb("eps", [P, 1])

        w1x = sb("w1x", [D, 2 * H])
        b1row = sb("b1row", [P, 2 * H])
        w1pe = sb("w1pe", [DE, H])
        w2f = sb("w2f", [H, D])
        w2p = sb("w2p", [H, D])
        b2frow = sb("b2frow", [P, D])
        b2pcol = sb("b2pcol", [D, 1])
        wc1a = sb("wc1a", [D, H])
        wc1b = sb("wc1b", [D, H])
        bc1col = sb("bc1col", [H, 1])
        wc2 = sb("wc2", [H, D])
        bc2col = sb("bc2col", [D, 1])
        wlr = sb("wlr", [D, 2, 2 * D])
        wlrT = sb("wlrT", [2 * D, 2, D])
        blcol = sb("blcol", [D, 2])

        src_i = sb("src_i", [P, GROUPS, TILES], I32)
        rel0 = sb("rel0", [P, GROUPS, TILES])
        rel = sb("rel", [P, GROUPS, TILES])
        base0 = sb("base0", [1, GROUPS])
        base = sb("base", [1, GROUPS])
        base_i = sb("base_i", [1, GROUPS], I32)
        gidx = sb("gidx", [P, 2, TILES], I32)
        rounds_i = sb("rounds_i", [1, 1], I32)

        s_const = sem("s_const")
        s_weights = sem("s_weights")
        s_iota = sem("s_iota")

        def weight_loads(sp):
            loads = [
                (w1x[:, 0:H], W1p[0:D, :]), (w1x[:, H:2 * H], W1f[0:D, :]),
                (b1row[:, 0:H], b1p.rearrange("(a n) -> a n", a=1).to_broadcast([P, H])),
                (b1row[:, H:2 * H], b1f.rearrange("(a n) -> a n", a=1).to_broadcast([P, H])),
                (w1pe[:, :], W1p[D:D + DE, :]),
                (w2f[:, :], W2f), (w2p[:, :], W2p),
                (b2frow[:, :], b2f.rearrange("(a n) -> a n", a=1).to_broadcast([P, D])),
                (b2pcol[:, :], b2p.rearrange("(n a) -> n a", a=1)),
                (wc1a[:, :], Wc1[0:D, :]), (wc1b[:, :], Wc1[D:2 * D, :]),
                (bc1col[:, :], bc1.rearrange("(n a) -> n a", a=1)),
                (wc2[:, :], Wc2), (bc2col[:, :], bc2.rearrange("(n a) -> n a", a=1)),
                (wlr[:, 0, 0:D], Wl0), (wlr[:, 0, D:2 * D], Wr0),
                (wlr[:, 1, 0:D], Wl1), (wlr[:, 1, D:2 * D], Wr1),
                (blcol[:, 0:1], bl0.rearrange("(n a) -> n a", a=1)),
                (blcol[:, 1:2], bl1.rearrange("(n a) -> n a", a=1)),
            ]
            for to, frm in loads:
                sp.dma_start(to, frm).then_inc(s_weights, 16)
            return 16 * len(loads)

        big = 4 * GROUP
        src_g = acc[0:98, 0:big].bitcast(I32).rearrange("p (c e) -> p c e", c=4)
        dst_g = acc[0:98, big:2 * big].bitcast(I32).rearrange("p (c e) -> p c e", c=4)
        src_f = acc[0:98, 2 * big:3 * big].rearrange("p (c e) -> p c e", c=4)
        dst_f = acc[0:98, 3 * big:4 * big].rearrange("p (c e) -> p c e", c=4)
        rel_f = acc[0:98, 4 * big:5 * big].rearrange("p (c e) -> p c e", c=4)
        low = acc[0:98, 5 * big:5 * big + 4]
        high = acc[0:98, 5 * big + 4:5 * big + 8]
        span = acc[0:98, 5 * big + 8:5 * big + 12]
        spans = cnt[0:1, 0:GROUPS]
        widest = cnt[0:1, 1000:1001]
        widest_i = cnt[0:1, 1001:1002].bitcast(I32)
        more_i = cnt[0:1, 1002:1003].bitcast(I32)
        lastrows = LOADS[3]
        parts = [(0, 98, 0, 3), (0, lastrows, 3, 4)]

        s_idx = sem("s_idx")
        s_float = sem("s_float")
        s_ext = sem("s_ext")
        s_rel = sem("s_rel")
        s_turn = sem("s_turn")
        s_turned = sem("s_turned")
        s_rowt = sem("s_rowt")
        s_row = sem("s_row")
        with nc.Block() as block:
            @block.sync
            def _(sp):
                n = 0
                for name, a, to in (("dst", dst, dst_g), ("src", src, src_g)):
                    g0 = 0
                    for c, size in enumerate(LOADS):
                        full = size - (c == 3)
                        sp.dma_start(to[0:full, c, :], a[g0 * GROUP:(g0 + full) * GROUP].rearrange(
                            "(g e) -> g e", e=GROUP)).then_inc(s_idx, 16)
                        g0 += size
                        n += 16
                    sp.dma_start(to[lastrows - 1:lastrows, 3, :],
                                 a[LAST:E].rearrange("(g e) -> g e", e=GROUP)).then_inc(s_idx, 16)
                    n += 16
                w = weight_loads(sp)
                sp.wait_ge(s_weights, w)

            @block.gpsimd
            def _(pool):
                nc.gpsimd.memset(ident[:, :], 0.0).then_inc(s_iota, 1)
                nc.gpsimd.memset(ident2[:, :], 0.0).then_inc(s_iota, 1)
                nc.gpsimd.memset(triu[:, :], 1.0).then_inc(s_iota, 1)
                nc.gpsimd.memset(ones[:, :], 1.0).then_inc(s_const, 1)
                nc.gpsimd.memset(mean[:, :], 1.0 / D).then_inc(s_const, 1)
                nc.gpsimd.memset(eps[:, :], EPS_LN).then_inc(s_const, 1)
                nc.gpsimd.iota(window_i[:, :], pattern=[[1, W]], base=0, channel_multiplier=0).then_inc(s_iota, 1)
                nc.gpsimd.iota(dump_i[:, :], pattern=[[0, 1]], base=N, channel_multiplier=1).then_inc(s_iota, 1)
                pool.wait_ge(s_iota, 5)
                nc.gpsimd.affine_select(out=ident[:, :], in_=ident[:, :], compare_op=ALU.not_equal, fill=1.0,
                                        base=0, pattern=[[-1, P]], channel_multiplier=1).then_inc(s_const, 1)
                nc.gpsimd.affine_select(out=ident2[:, :], in_=ident2[:, :], compare_op=ALU.not_equal, fill=2.0,
                                        base=0, pattern=[[-1, P]], channel_multiplier=1).then_inc(s_const, 1)
                nc.gpsimd.affine_select(out=triu[:, :], in_=triu[:, :], compare_op=ALU.is_ge, fill=0.0,
                                        base=0, pattern=[[1, P]], channel_multiplier=-1).then_inc(s_const, 1)
                nc.gpsimd.tensor_copy(window[:, :], window_i[:, :]).then_inc(s_const, 1)
                nc.gpsimd.tensor_copy(dump[:, :], dump_i[:, :]).then_inc(s_const, 1)

            @block.vector
            def _(dve):
                dve.wait_ge(s_idx, 16 * 10)
                for p0, p1, c0, c1 in parts:
                    dve.tensor_copy(dst_f[p0:p1, c0:c1, :], dst_g[p0:p1, c0:c1, :]).then_inc(s_float, 1)
                    dve.tensor_copy(src_f[p0:p1, c0:c1, :], src_g[p0:p1, c0:c1, :]).then_inc(s_float, 1)
                dve.wait_ge(s_float, 4)
                for p0, p1, c0, c1 in parts:
                    dve.tensor_reduce(low[p0:p1, c0:c1], dst_f[p0:p1, c0:c1, :], AX_X, ALU.min).then_inc(s_ext, 1)
                    dve.tensor_reduce(high[p0:p1, c0:c1], dst_f[p0:p1, c0:c1, :], AX_X, ALU.max).then_inc(s_ext, 1)
                dve.wait_ge(s_ext, 4)
                for c in range(4):
                    dve.tensor_scalar(rel_f[0:LOADS[c], c, :], dst_f[0:LOADS[c], c, :], low[0:LOADS[c], c:c + 1],
                                      None, ALU.subtract).then_inc(s_rel, 1)
                for p0, p1, c0, c1 in parts:
                    dve.tensor_tensor(span[p0:p1, c0:c1], high[p0:p1, c0:c1], low[p0:p1, c0:c1],
                                      ALU.subtract).then_inc(s_rel, 1)
                k = 0
                g0 = 0
                for c, size in enumerate(LOADS):
                    for to in (rel0, src_i):
                        dve.wait_ge(s_turn, k + 1)
                        t = bank[k % 2][:, 0:TILES * size].rearrange("p (q g) -> p q g", q=TILES)
                        dve.tensor_copy(to[:, g0:g0 + size, :].rearrange("p g q -> p q g"), t).then_inc(s_turned, 1)
                        k += 1
                    g0 += size
                dve.wait_ge(s_turned, 8)
                dve.memset(rel0[0:OVERLAP // TILES, GROUPS - 1, :], -1.0e6)
                dve.wait_ge(s_rowt, 1)
                dve.tensor_copy(base0[:, :], bank[2][0:1, 0:GROUPS])
                dve.tensor_copy(spans, bank[3][0:1, 0:GROUPS]).then_inc(s_row, 1)
                dve.wait_ge(s_row, 1)
                dve.tensor_reduce(widest, spans, AX_X, ALU.max).then_inc(s_row, 1)
                dve.wait_ge(s_row, 2)
                dve.tensor_copy(widest_i, widest).then_inc(s_row, 1)
                dve.wait_ge(s_row, 3)
                dve.tensor_single_scalar(more_i, widest_i, W.bit_length() - 1, ALU.logical_shift_right).then_inc(s_row, 1)
                dve.wait_ge(s_row, 4)
                dve.tensor_scalar(rounds_i[:, :], more_i, 1, None, ALU.add).then_inc(s_row, 1)

            @block.tensor
            def _(pe):
                pe.wait_ge(s_const, 8)
                pe.wait_ge(s_rel, 6)
                k = 0
                for c, size in enumerate(LOADS):
                    for frm in (rel_f, src_f):
                        if k >= 2:
                            pe.wait_ge(s_turned, k - 1)
                        for q in range(TILES):
                            v = frm[0:size, c, :].rearrange("g (p q) -> g q p", q=TILES)
                            last = pe.transpose(bank[k % 2][:, q * size:(q + 1) * size], v[:, q, :],
                                                ident[0:size, 0:size])
                        last.then_inc(s_turn, 1)
                        k += 1
                g0 = 0
                for c, size in enumerate(LOADS):
                    pe.transpose(bank[2][0:1, g0:g0 + size], low[0:size, c:c + 1], ident[0:size, 0:size])
                    last = pe.transpose(bank[3][0:1, g0:g0 + size], span[0:size, c:c + 1], ident[0:size, 0:size])
                    g0 += size
                last.then_inc(s_rowt, 1)

        xin = sb("xin", [CP, 2, CQ * D])
        chunkT = tmp("chunkT", [D, 2, CH])
        table = tmp("table", [CP, 2, CQ, 2 * H])
        x_c = x.rearrange("(c p q) d -> c p (q d)", p=CP, q=CQ)
        Ap_c = Ap.rearrange("(c p q) h -> c p q h", p=CP, q=CQ)
        Af_c = Af[0:N, :].rearrange("(c p q) h -> c p q h", p=CP, q=CQ)

        sA_x = [sem(f"sA_x{b}") for b in range(2)]
        sA_store = [sem(f"sA_store{b}") for b in range(2)]
        sA_zero = sem("sA_zero")
        sA_zeroed = sem("sA_zeroed")
        sA_t = sem("sA_t")
        sA_T = sem("sA_T")
        sA_h = sem("sA_h")
        sA_tab = sem("sA_tab")
        with nc.Block() as block:
            @block.sync
            def _(sp):
                for c in range(CHUNKS):
                    b = c % 2
                    if c >= 2:
                        sp.wait_ge(sA_t, c - 1)
                    sp.dma_start(xin[:, b, :], x_c[c]).then_inc(sA_x[b], 16)

            @block.scalar
            def _(act):
                for c in range(CHUNKS):
                    act.wait_ge(sA_t, c + 1)
                    if c >= 2:
                        act.wait_ge(sA_h, c - 1)
                    act.copy(chunkT[:, c % 2, :], bank[c % 2][0:D, 0:CH]).then_inc(sA_T, 1)

            @block.tensor
            def _(pe):
                for l in range(2):
                    pe.transpose(bank[6][:, l * D:(l + 1) * D], wlr[:, l, :], ident[0:D, 0:D])
                for c in range(CHUNKS + 1):
                    if c < CHUNKS:
                        b = c % 2
                        pe.wait_ge(sA_x[b], 16 * (c // 2 + 1))
                        if c >= 2:
                            pe.wait_ge(sA_T, c - 1)
                        for q in range(CQ):
                            last = pe.transpose(bank[b][0:D, q * CP:(q + 1) * CP],
                                                xin[:, b, q * D:(q + 1) * D], ident[0:CP, 0:CP])
                        last.then_inc(sA_t, 1)
                    if c >= 1:
                        k = c - 1
                        b = k % 2
                        pe.wait_ge(sA_T, k + 1)
                        if k >= 2:
                            pe.wait_ge(sA_tab, 2 * (k - 1))
                        for q in range(CQ):
                            last = pe.matmul(bank[2 + 2 * b + q // 2][0:CP, (q % 2) * 256:(q % 2) * 256 + 256],
                                             chunkT[:, b, q * CP:(q + 1) * CP], w1x[:, :], start=True, stop=True)
                        last.then_inc(sA_h, 1)

            @block.vector
            def _(dve):
                dve.memset(acc[:, :], 0.0).then_inc(sA_zero, 1)
                dve.memset(cnt[:, :], 0.0)
                dve.tensor_copy(rel[:, :, :], rel0[:, :, :])
                dve.tensor_copy(base[:, :], base0[:, :])
                dve.wait_ge(sA_h, 1)
                dve.tensor_copy(wlrT[:, :, :], bank[6][:, 0:2 * D].rearrange("p (l d) -> p l d", l=2))
                for c in range(CHUNKS):
                    b = c % 2
                    dve.wait_ge(sA_h, c + 1)
                    if c >= 2:
                        dve.wait_ge(sA_store[b], 32 * (c // 2))
                    for h in range(2):
                        dve.tensor_tensor(
                            table[:, b, 2 * h:2 * h + 2, :],
                            bank[2 + 2 * b + h][0:CP, :].rearrange("p (q n) -> p q n", q=2),
                            b1row[0:CP, :].unsqueeze(1).to_broadcast([CP, 2, 2 * H]), ALU.add).then_inc(sA_tab, 1)

            @block.gpsimd
            def _(pool):
                pool.wait_ge(sA_zero, 1)
                for q in range(TILES):
                    pool.dma_start(future[q].rearrange("(p r) d -> p (r d)", p=P), acc[:, 0:ZCOLS]).then_inc(sA_zeroed, 16)
                pool.dma_start(Af[N:NW, :], acc[0:W, 0:H]).then_inc(sA_zeroed, 16)
                for c in range(CHUNKS):
                    b = c % 2
                    pool.wait_ge(sA_tab, 2 * (c + 1))
                    pool.dma_start(Ap_c[c], table[:, b, :, 0:H]).then_inc(sA_store[b], 16)
                    pool.dma_start(Af_c[c], table[:, b, :, H:2 * H]).then_inc(sA_store[b], 16)
                pool.wait_ge(sA_zeroed, 16 * (TILES + 1))
                pool.wait_ge(sA_store[0], 32 * ((CHUNKS + 1) // 2))
                pool.wait_ge(sA_store[1], 32 * (CHUNKS // 2))

        next_stage()

        rounds = nc.values_load(rounds_i[0:1, 0:1], min_val=1, max_val=N // W + 1)

        srcm = tmp("srcm", [P, GROUPS, TILES])
        inwin = tmp("inwin", [P, GROUPS, TILES])
        comb = tmp("comb", [P, 2, TILES, DE + W])
        wwin = tmp("wwin", [DE + W, 2, H])
        gbuf = tmp("gbuf", [P, 2, TILES, H])
        skey = tmp("skey", [P, 2, TILES])
        equal = tmp("equal", [P, 2, TILES, P])
        later = tmp("later", [P, 2, TILES])
        away = tmp("away", [P, 2, TILES])
        pick = tmp("pick", [P, 2, TILES])
        sidx = tmp("sidx", [P, 2, TILES], I32)
        featT = tmp("featT", [DE + W, 2, GROUP])
        hidf = tmp("hidf", [H, 2, GROUP])
        msg = tmp("msg", [P, 2, TILES, D])
        sbuf = tmp("sbuf", [P, 2, TILES, D])
        pre = tmp("pre", [P, 2, GROUP])
        hidp = tmp("hidp", [P, 2, GROUP])

        psR, psT, psF, psP, psM, psD, psS = bank[0:7]

        edge_sems = {}

        def esem(name):
            edge_sems[name] = sem(name)
            return edge_sems[name]

        s_prep = esem("s_prep")
        s_wedge = esem("s_wedge")
        s_ea = [esem(f"s_ea{b}") for b in range(2)]
        s_win = [esem(f"s_win{b}") for b in range(2)]
        s_gat = [esem(f"s_gat{b}") for b in range(2)]
        s_sc = [esem(f"s_sc{q}") for q in range(TILES)]
        s_open = esem("s_open")
        s_scdone = esem("s_scdone")
        s_gidx = esem("s_gidx")
        s_sm = esem("s_sm")
        s_oh = esem("s_oh")
        s_eu = esem("s_eu")
        s_away = esem("s_away")
        s_pick = esem("s_pick")
        s_sidx = esem("s_sidx")
        s_msb = esem("s_msb")
        s_pre = esem("s_pre")
        s_acc = esem("s_acc")
        s_stk = esem("s_stk")
        s_slope = esem("s_slope")
        s_hf = esem("s_hf")
        s_hp = esem("s_hp")
        s_sb = esem("s_sb")
        s_R = esem("s_R")
        s_T = esem("s_T")
        s_F = esem("s_F")
        s_P = esem("s_P")
        s_M = esem("s_M")
        s_D = esem("s_D")
        s_S = esem("s_S")

        def over_groups(eng, step, first=0):
            step(0, 0, 0, True)
            step(1, 0, 1, True)
            with eng.Fori(1, PAIRS) as i:
                step(2 * i, i, 0, False)
                step(2 * i + 1, i, 1, False)
            step(GROUPS - 1, PAIRS, 0, False)

        def final(g):
            return isinstance(g, int) and g == GROUPS - 1

        def windows(dve, done):
            dve.tensor_scalar(base_i[:, :], base[:, :], float(N), None, ALU.min).then_inc(done, 1)

        def next_windows(dve):
            dve.tensor_scalar(rel[:, :, :], rel[:, :, :], -float(W), None, ALU.add)
            dve.tensor_scalar(base[:, :], base[:, :], float(W), None, ALU.add)

        ea_main = ea[0:(GROUPS - 1) * GROUP, :].rearrange("(g p q) f -> g p q f", p=P, q=TILES)
        ea_last = ea[LAST:E, :].rearrange("(p q) f -> p q f", q=TILES)
        window_b = window[:, :].unsqueeze(1).to_broadcast([P, TILES, W])

        with nc.Fori(0, rounds):
            with nc.Block() as block:
                @block.sync
                def _(sp):
                    for b in range(2):
                        sp.dma_start(wwin[0:DE, b, :], W1f[D:D + DE, :]).then_inc(s_wedge, 16)
                    sp.wait_ge(s_prep, 4)

                    def step(g, pair, b, early):
                        if not early:
                            sp.wait_ge(s_T, g - 1)
                        sp.dma_start(comb[:, b, :, 0:DE], ea_last if final(g) else ea_main[g]).then_inc(s_ea[b], 16)
                        row = sp.value_load(base_i[0:1, g:g + 1] if isinstance(g, int)
                                            else base_i[0:1, bass.DynSlice(g, 1)], min_val=0, max_val=N)
                        if not early:
                            sp.wait_ge(s_F, g - 1)
                        sp.dma_start(wwin[DE:DE + W, b, :], Af[bass.DynSlice(row, W), :]).then_inc(s_win[b], 16)

                    over_groups(sp, step)

                @block.gpsimd
                def _(pool):
                    def gathers(b):
                        for q in range(TILES):
                            pool.indirect_dma_start(
                                out=gbuf[:, b, q, :], out_offset=None, in_=Ap[:, :],
                                in_offset=bass.IndirectOffsetOnAxis(ap=gidx[:, b, q:q + 1], axis=0)).then_inc(s_gat[b], 16)

                    pool.wait_ge(s_gidx, 1)
                    gathers(0)

                    def step(g, pair, b, early):
                        if not final(g):
                            if not (isinstance(g, int) and g == 0):
                                pool.wait_ge(s_pre, g)
                            pool.wait_ge(s_gidx, g + 2)
                            pool.sem_inc(s_open, 1)
                            gathers(1 - b)
                        if not (isinstance(g, int) and g == 0):
                            for q in range(TILES):
                                pool.wait_ge(s_sc[q], 16 * g)
                        pool.wait_ge(s_sidx, g + 1)
                        pool.wait_ge(s_sb, g + 1)
                        pool.sem_inc(s_scdone, 1)
                        for q in range(TILES):
                            pool.indirect_dma_start(
                                out=future[q][:, :],
                                out_offset=bass.IndirectOffsetOnAxis(ap=sidx[:, b, q:q + 1], axis=0),
                                in_=sbuf[:, b, q, :], in_offset=None, compute_op=ALU.add).then_inc(s_sc[q], 16)

                    over_groups(pool, step)
                    for q in range(TILES):
                        pool.wait_ge(s_sc[q], 16 * GROUPS)

                @block.vector
                def _(dve):
                    windows(dve, s_prep)
                    dve.tensor_single_scalar(inwin[:, :, :], rel[:, :, :], 0.0, ALU.is_ge).then_inc(s_prep, 1)
                    dve.tensor_scalar(srcm[:, :, :], src_i[:, :, :], dump[:, 0:1], None, ALU.subtract).then_inc(s_prep, 1)
                    dve.wait_ge(s_prep, 3)
                    dve.scalar_tensor_tensor(out=inwin[:, :, :], in0=rel[:, :, :], scalar=float(W), in1=inwin[:, :, :],
                                             op0=ALU.is_lt, op1=ALU.mult).then_inc(s_prep, 1)
                    dve.wait_ge(s_prep, 4)
                    dve.tensor_tensor(srcm[:, :, :], srcm[:, :, :], inwin[:, :, :], ALU.mult).then_inc(s_prep, 1)
                    dve.wait_ge(s_prep, 5)
                    dve.tensor_scalar(srcm[:, :, :], srcm[:, :, :], dump[:, 0:1], None, ALU.add).then_inc(s_prep, 1)
                    dve.tensor_copy(gidx[:, 0, :], src_i[:, 0, :]).then_inc(s_gidx, 1)
                    dve.wait_ge(s_prep, 6)

                    def col(t, g):
                        return t[:, g, :] if isinstance(g, int) else t[:, bass.DynSlice(g, 1), :].rearrange("p a q -> p (a q)")

                    def add_sums(g):
                        at = dve.value_load(base_i[0:1, g:g + 1] if isinstance(g, int)
                                            else base_i[0:1, bass.DynSlice(g, 1)], min_val=0, max_val=N)
                        if not (isinstance(g, int) and g == 0):
                            dve.wait_ge(s_acc, 2 * g)
                        dve.wait_ge(s_S, g + 1)
                        v = acc[:, bass.DynSlice(at, W)]
                        dve.tensor_tensor(v, v, psS[:, 0:W], ALU.add).then_inc(s_acc, 1)
                        v = cnt[:, bass.DynSlice(at, W)]
                        dve.tensor_tensor(v, v, psS[0:D, W:2 * W], ALU.add).then_inc(s_acc, 1)

                    def step(g, pair, b, early):
                        if not final(g):
                            dve.tensor_copy(gidx[:, 1 - b, :], col(src_i, g + 1)).then_inc(s_gidx, 1)
                        if not early:
                            dve.wait_ge(s_R, g - 1)
                        dve.tensor_copy(skey[:, b, :], col(srcm, g)).then_inc(s_sm, 1)
                        if not early:
                            dve.wait_ge(s_S, g - 1)
                        dve.tensor_tensor(comb[:, b, :, DE:DE + W], window_b,
                                          col(rel, g).unsqueeze(2).to_broadcast([P, TILES, W]),
                                          ALU.is_equal).then_inc(s_oh, 1)
                        dve.wait_ge(s_sm, g + 1)
                        dve.tensor_scalar(away[:, b, :], skey[:, b, :], dump[:, 0:1], None, ALU.subtract).then_inc(s_away, 1)
                        if not early:
                            dve.wait_ge(s_D, g - 1)
                        dve.wait_ge(s_R, g + 1)
                        for q in range(TILES):
                            dve.scalar_tensor_tensor(out=equal[:, b, q, :], in0=psR[:, q * P:(q + 1) * P],
                                                     scalar=skey[:, b, q:q + 1], in1=triu[:, :],
                                                     op0=ALU.is_equal, op1=ALU.mult,
                                                     accum_out=later[:, b, q:q + 1]).then_inc(s_eu, 1)
                        if not (isinstance(g, int) and g == 0):
                            add_sums(g - 1)
                        dve.wait_ge(s_away, g + 1)
                        dve.wait_ge(s_eu, 4 * g + 4)
                        dve.scalar_tensor_tensor(out=pick[:, b, :], in0=later[:, b, :], scalar=1.0, in1=away[:, b, :],
                                                 op0=ALU.is_equal, op1=ALU.mult).then_inc(s_pick, 1)
                        if not early:
                            dve.wait_ge(s_scdone, g)
                        dve.wait_ge(s_pick, g + 1)
                        dve.tensor_scalar(sidx[:, b, :], pick[:, b, :], dump[:, 0:1], None, ALU.add).then_inc(s_sidx, 1)
                        dve.wait_ge(s_slope, g + 1)
                        dve.tensor_tensor(hidf[:, b, :], hidf[:, b, :], psF[:, :], ALU.max).then_inc(s_hf, 1)
                        dve.wait_ge(s_gat[b], 64 * pair + 64)
                        dve.wait_ge(s_P, g + 1)
                        dve.tensor_tensor(pre[:, b, :], psP[:, :], gbuf[:, b, :, :].rearrange("p q h -> p (q h)"),
                                          ALU.add).then_inc(s_pre, 1)
                        dve.wait_ge(s_M, g + 1)
                        dve.tensor_tensor(msg[:, b, :, :], psM[:, 0:TILES * D].rearrange("p (q d) -> p q d", q=TILES),
                                          b2frow[:, :].unsqueeze(1).to_broadcast([P, TILES, D]),
                                          ALU.add).then_inc(s_msb, 1)
                        dve.wait_ge(s_pre, g + 1)
                        dve.scalar_tensor_tensor(out=hidp[:, b, :], in0=pre[:, b, :], scalar=SLOPE, in1=pre[:, b, :],
                                                 op0=ALU.mult, op1=ALU.max).then_inc(s_hp, 1)

                    over_groups(dve, step)
                    add_sums(GROUPS - 1)
                    next_windows(dve)

                @block.scalar
                def _(act):
                    def step(g, pair, b, early):
                        if not early:
                            act.wait_ge(s_P, g - 1)
                        act.wait_ge(s_T, g + 1)
                        act.copy(featT[:, b, :], psT[0:DE + W, :]).then_inc(s_stk, 1)
                        if not early:
                            act.wait_ge(s_M, g - 1)
                        act.wait_ge(s_F, g + 1)
                        act.activation(hidf[:, b, :], psF[:, :], ACT.Copy, scale=SLOPE).then_inc(s_slope, 1)
                        if not early:
                            act.wait_ge(s_scdone, g)
                        act.wait_ge(s_D, g + 1)
                        act.copy(sbuf[:, b, :, :], psD[:, 0:TILES * D].rearrange("p (q d) -> p q d", q=TILES)).then_inc(s_sb, 1)

                    over_groups(act, step)

                @block.tensor
                def _(pe):
                    def sums(g, b):
                        if not (isinstance(g, int) and g == 0):
                            pe.wait_ge(s_acc, 2 * g)
                        pe.wait_ge(s_hp, g + 1)
                        for q in range(TILES):
                            pe.matmul(psS[:, 0:W], hidp[:, b, q * P:(q + 1) * P], comb[:, b, q, DE:DE + W],
                                      start=(q == 0), stop=(q == TILES - 1))
                        for q in range(TILES):
                            last = pe.matmul(psS[0:D, W:2 * W], ones[:, :], comb[:, b, q, DE:DE + W],
                                             start=(q == 0), stop=(q == TILES - 1))
                        last.then_inc(s_S, 1)

                    pe.wait_ge(s_wedge, 32)

                    def step(g, pair, b, early):
                        first = isinstance(g, int) and g == 0
                        if not first:
                            pe.wait_ge(s_eu, 4 * g)
                        pe.wait_ge(s_sm, g + 1)
                        for q in range(TILES):
                            last = pe.transpose(psR[:, q * P:(q + 1) * P],
                                                skey[:, b, q:q + 1].to_broadcast([P, P]), ident[:, :])
                        last.then_inc(s_R, 1)
                        pe.wait_ge(s_ea[b], 16 * pair + 16)
                        if not first:
                            pe.wait_ge(s_stk, g)
                        pe.wait_ge(s_oh, g + 1)
                        for q in range(TILES):
                            last = pe.transpose(psT[0:DE + W, q * P:(q + 1) * P], comb[:, b, q, :], ident[:, :])
                        last.then_inc(s_T, 1)
                        if not first:
                            sums(g - 1, 1 - b)
                        pe.wait_ge(s_win[b], 16 * pair + 16)
                        if not first:
                            pe.wait_ge(s_hf, g)
                        pe.wait_ge(s_stk, g + 1)
                        pe.matmul(psF[:, :], wwin[:, b, :], featT[:, b, :], start=True, stop=True).then_inc(s_F, 1)
                        if not first:
                            pe.wait_ge(s_pre, g)
                        for q in range(TILES):
                            last = pe.matmul(psP[:, q * H:(q + 1) * H], featT[0:DE, b, q * P:(q + 1) * P], w1pe[:, :],
                                             start=True, stop=True)
                        last.then_inc(s_P, 1)
                        if not first:
                            pe.wait_ge(s_msb, g)
                        pe.wait_ge(s_hf, g + 1)
                        for q in range(TILES):
                            last = pe.matmul(psM[:, q * D:(q + 1) * D], hidf[:, b, q * P:(q + 1) * P], w2f[:, :],
                                             start=True, stop=True)
                        last.then_inc(s_M, 1)
                        if not first:
                            pe.wait_ge(s_sb, g)
                        pe.wait_ge(s_eu, 4 * g + 4)
                        pe.wait_ge(s_msb, g + 1)
                        for q in range(TILES):
                            last = pe.matmul(psD[:, q * D:(q + 1) * D], equal[:, b, q, :], msg[:, b, q, :],
                                             start=True, stop=True)
                        last.then_inc(s_D, 1)

                    over_groups(pe, step)
                    sums(GROUPS - 1, 0)

            for s in edge_sems.values():
                nc.sync.sem_clear(s)
            nc.all_engine_barrier()

        next_stage()

        def by_slot(t, c):
            return t[:, c * CH:(c + 1) * CH].rearrange("k (p q) -> k q p", q=CQ)

        def cols(t):
            return t.rearrange("k (q p) -> k q p", q=CQ)

        fut = sb("fut", [CP, 2, TILES, CQ * D])
        fsum = sb("fsum", [CP, 2, CQ * D])
        nT = [sb(f"nT{i}", [D, 2, CH]) for i in range(6)]
        hidc = sb("hidc", [H, 2, CH])
        rows = sb("rows", [CP, 2, CQ * D])
        past_b, flow_b, futT_b, y_b, yc_b, sq_b = nT
        future_c = [f[0:N, :].rearrange("(c p q) d -> c p (q d)", p=CP, q=CQ) for f in future]
        x1_c = x1.rearrange("(c p q) d -> c p (q d)", p=CP, q=CQ)
        h1_c = h1.rearrange("(c p q) d -> c p (q d)", p=CP, q=CQ)
        out_c = out.rearrange("(c p q) d -> c p (q d)", p=CP, q=CQ)

        sC_in = [sem(f"sC_in{b}") for b in range(2)]
        sC_st = [sem(f"sC_st{b}") for b in range(2)]
        (sC_v, sC_v2, sC_fs, sC_flow, sC_yc, sC_x1, sC_fT, sC_hc, sC_y, sC_sq, sC_sd, sC_row,
         sC_P, sC_F, sC_H, sC_O, sC_m, sC_s, sC_N, sC_act) = [sem(f"sC_{i}") for i in range(20)]
        with nc.Block() as block:
            @block.sync
            def _(sp):
                for c in range(CHUNKS + 1):
                    if c < CHUNKS:
                        b = c % 2
                        if c >= 2:
                            sp.wait_ge(sC_O, c - 1)
                            sp.wait_ge(sC_fs, c - 1)
                        sp.dma_start(xin[:, b, :], x_c[c]).then_inc(sC_in[b], 16)
                        for k in range(TILES):
                            sp.dma_start(fut[:, b, k, :], future_c[k][c]).then_inc(sC_in[b], 16)
                    if c >= 1:
                        k = c - 1
                        sp.wait_ge(sC_x1, k + 1)
                        sp.dma_start(x1T[k], y_b[:, k % 2, :]).then_inc(sC_st[k % 2], 16)
                        sp.wait_ge(sC_row, k + 1)
                        sp.dma_start(x1_c[k], rows[:, k % 2, :]).then_inc(sC_st[k % 2], 16)
                sp.wait_ge(sC_st[0], 32 * ((CHUNKS + 1) // 2))
                sp.wait_ge(sC_st[1], 32 * (CHUNKS // 2))

            @block.vector
            def _(dve):
                v = [0]

                def link(ins):
                    v[0] += 1
                    ins.then_inc(sC_v, 1)
                    dve.wait_ge(sC_v, v[0])

                for c in range(CHUNKS):
                    b = c % 2
                    dve.wait_ge(sC_in[b], 80 * (c // 2 + 1))
                    if c >= 2:
                        dve.wait_ge(sC_F, c - 1)
                    link(dve.tensor_tensor(fsum[:, b, :], fut[:, b, 0, :], fut[:, b, 1, :], ALU.add))
                    link(dve.tensor_tensor(fsum[:, b, :], fsum[:, b, :], fut[:, b, 2, :], ALU.add))
                    dve.tensor_tensor(fsum[:, b, :], fsum[:, b, :], fut[:, b, 3, :], ALU.add).then_inc(sC_fs, 1)
                    dve.wait_ge(sC_P, c + 1)
                    link(dve.scalar_tensor_tensor(out=cols(past_b[:, b, :]), in0=by_slot(cnt, c), scalar=b2pcol[:, 0:1],
                                                  in1=cols(bank[0][0:D, 0:CH]), op0=ALU.mult, op1=ALU.add))
                    n = cnt[:, c * CH:(c + 1) * CH]
                    link(dve.tensor_scalar(n, n, 1.0, None, ALU.max))
                    link(dve.reciprocal(n, n))
                    if c >= 2:
                        dve.wait_ge(sC_H, c - 1)
                    dve.tensor_tensor(cols(flow_b[:, b, :]), cols(past_b[:, b, :]), by_slot(cnt, c), ALU.mult).then_inc(sC_flow, 1)
                    dve.wait_ge(sC_hc, c + 1)
                    dve.scalar_tensor_tensor(out=hidc[:, b, :], in0=hidc[:, b, :], scalar=SLOPE, in1=hidc[:, b, :],
                                             op0=ALU.mult, op1=ALU.max).then_inc(sC_act, 1)
                    dve.wait_ge(sC_m, c + 1)
                    dve.tensor_tensor(yc_b[:, b, :], y_b[:, b, :], bank[4][0:D, 0:CH], ALU.subtract).then_inc(sC_yc, 1)
                    dve.wait_ge(sC_sd, c + 1)
                    link(dve.reciprocal(sq_b[:, b, :], sq_b[:, b, :]))
                    dve.wait_ge(sC_yc, c + 1)
                    dve.tensor_tensor(y_b[:, b, :], yc_b[:, b, :], sq_b[:, b, :], ALU.mult).then_inc(sC_x1, 1)
                dve.wait_ge(sC_P, CHUNKS)
                dve.memset(acc[0:D, :], 0.0)
                dve.tensor_copy(rel[:, :, :], rel0[:, :, :])
                dve.tensor_copy(base[:, :], base0[:, :])

            @block.scalar
            def _(act):
                for c in range(CHUNKS):
                    b = c % 2
                    act.wait_ge(sC_F, c + 1)
                    if c >= 2:
                        act.wait_ge(sC_H, c - 1)
                    act.copy(futT_b[:, b, :], bank[1][0:D, 0:CH]).then_inc(sC_fT, 1)
                    act.wait_ge(sC_H, c + 1)
                    if c >= 2:
                        act.wait_ge(sC_O, c - 1)
                    act.activation(hidc[:, b, :], bank[2][:, 0:CH], ACT.Identity, bias=bc1col[:, 0:1]).then_inc(sC_hc, 1)
                    act.wait_ge(sC_O, c + 1)
                    if c >= 2:
                        act.wait_ge(sC_st[b], 32 * (c // 2))
                        act.wait_ge(sC_N, c - 1)
                    act.activation(y_b[:, b, :], bank[3][0:D, 0:CH], ACT.Identity, bias=bc2col[:, 0:1]).then_inc(sC_y, 1)
                    act.wait_ge(sC_yc, c + 1)
                    if c >= 2:
                        act.wait_ge(sC_x1, c - 1)
                    act.activation(sq_b[:, b, :], yc_b[:, b, :], ACT.Square).then_inc(sC_sq, 1)
                    act.wait_ge(sC_s, c + 1)
                    act.activation(sq_b[:, b, :], bank[5][0:D, 0:CH], ACT.Sqrt, bias=eps[0:D, 0:1]).then_inc(sC_sd, 1)
                    act.wait_ge(sC_N, c + 1)
                    act.copy(rows[:, b, :], bank[6][0:CP, 0:CQ * D]).then_inc(sC_row, 1)

            @block.tensor
            def _(pe):
                for c in range(CHUNKS):
                    b = c % 2
                    if c >= 1:
                        pe.wait_ge(sC_flow, c)
                    pe.matmul(bank[0][0:D, 0:CH].rearrange("k (q p) -> k q p", q=CQ), w2p[:, :], by_slot(acc, c),
                              start=True, stop=True).then_inc(sC_P, 1)
                    pe.wait_ge(sC_fs, c + 1)
                    if c >= 1:
                        pe.wait_ge(sC_fT, c)
                    for q in range(CQ):
                        last = pe.transpose(bank[1][0:D, q * CP:(q + 1) * CP], fsum[:, b, q * D:(q + 1) * D],
                                            ident[0:CP, 0:CP])
                    last.then_inc(sC_F, 1)
                    pe.wait_ge(sC_flow, c + 1)
                    pe.wait_ge(sC_fT, c + 1)
                    if c >= 1:
                        pe.wait_ge(sC_hc, c)
                    pe.matmul(bank[2][:, 0:CH], wc1a[:, :], flow_b[:, b, :], start=True, stop=False)
                    pe.matmul(bank[2][:, 0:CH], wc1b[:, :], futT_b[:, b, :], start=False, stop=True).then_inc(sC_H, 1)
                    pe.wait_ge(sC_in[b], 80 * (c // 2 + 1))
                    pe.wait_ge(sC_act, c + 1)
                    if c >= 1:
                        pe.wait_ge(sC_y, c)
                    pe.matmul(bank[3][0:D, 0:CH], wc2[:, :], hidc[:, b, :], start=True, stop=False, skip_group_check=True)
                    for q in range(CQ):
                        last = pe.matmul(bank[3][0:D, q * CP:(q + 1) * CP], xin[:, b, q * D:(q + 1) * D],
                                         ident2[0:CP, 0:CP], start=False, stop=(q == CQ - 1), skip_group_check=True)
                    last.then_inc(sC_O, 1)
                    pe.wait_ge(sC_y, c + 1)
                    pe.matmul(bank[4][0:D, 0:CH], mean[:, :], y_b[:, b, :], start=True, stop=True).then_inc(sC_m, 1)
                    pe.wait_ge(sC_sq, c + 1)
                    pe.matmul(bank[5][0:D, 0:CH], mean[:, :], sq_b[:, b, :], start=True, stop=True).then_inc(sC_s, 1)
                    pe.wait_ge(sC_x1, c + 1)
                    for q in range(CQ):
                        last = pe.transpose(bank[6][0:CP, q * D:(q + 1) * D], y_b[:, b, q * CP:(q + 1) * CP],
                                            ident[0:D, 0:D])
                    last.then_inc(sC_N, 1)

        kst = sb("kst", [2 * D, 2, CH])
        oneh = sb("oneh", [P, 2, TILES, W])
        gb1 = sb("gb1", [P, 2, TILES, D])
        h_b, hs_b, n_b, ho_b, x1c_b, yy_b = nT

        for layer in range(2):
            frm = (x1, h1)[layer]
            frmT = (x1T, h1T)[layer]
            L = f"L{layer}_"
            layer_sems = []

            def lsem(name):
                layer_sems.append(sem(L + name))
                return layer_sems[-1]

            t_prep = lsem("prep")
            t_gat = [lsem(f"gat{b}") for b in range(2)]
            t_gidx = lsem("gidx")
            t_open = lsem("open")
            t_oh = lsem("oh")
            t_S = lsem("S")
            t_acc = lsem("acc")
            with nc.Fori(0, rounds):
                with nc.Block() as block:
                    @block.gpsimd
                    def _(pool):
                        def step(g, pair, b, early):
                            pool.wait_ge(t_gidx, g + 1)
                            if not early:
                                pool.wait_ge(t_S, g - 1)
                            pool.sem_inc(t_open, 1)
                            for q in range(TILES):
                                pool.indirect_dma_start(
                                    out=gb1[:, b, q, :], out_offset=None, in_=frm[:, :],
                                    in_offset=bass.IndirectOffsetOnAxis(ap=gidx[:, b, q:q + 1], axis=0)).then_inc(t_gat[b], 16)

                        over_groups(pool, step)

                    @block.vector
                    def _(dve):
                        windows(dve, t_prep)
                        dve.wait_ge(t_prep, 1)

                        def col(t, g):
                            return t[:, g, :] if isinstance(g, int) else t[:, bass.DynSlice(g, 1), :].rearrange("p a q -> p (a q)")

                        def add_sums(g, b):
                            at = dve.value_load(base_i[0:1, g:g + 1] if isinstance(g, int)
                                                else base_i[0:1, bass.DynSlice(g, 1)], min_val=0, max_val=N)
                            if not (isinstance(g, int) and g == 0):
                                dve.wait_ge(t_acc, g)
                            dve.wait_ge(t_S, g + 1)
                            v = acc[0:D, bass.DynSlice(at, W)]
                            dve.tensor_tensor(v, v, bank[b][0:D, 0:W], ALU.add).then_inc(t_acc, 1)

                        def step(g, pair, b, early):
                            if not early:
                                dve.wait_ge(t_S, g - 1)
                            dve.tensor_copy(gidx[:, b, :], col(src_i, g)).then_inc(t_gidx, 1)
                            dve.tensor_tensor(oneh[:, b, :, :], window_b,
                                              col(rel, g).unsqueeze(2).to_broadcast([P, TILES, W]),
                                              ALU.is_equal).then_inc(t_oh, 1)
                            if not (isinstance(g, int) and g == 0):
                                add_sums(g - 1, 1 - b)

                        over_groups(dve, step)
                        add_sums(GROUPS - 1, 0)
                        next_windows(dve)

                    @block.tensor
                    def _(pe):
                        def step(g, pair, b, early):
                            if not early:
                                pe.wait_ge(t_acc, g - 1)
                            pe.wait_ge(t_oh, g + 1)
                            pe.wait_ge(t_gat[b], 64 * pair + 64)
                            pe.sem_inc(t_open, 1)
                            for q in range(TILES):
                                last = pe.matmul(bank[b][0:D, 0:W], gb1[:, b, q, :], oneh[:, b, q, :],
                                                 start=(q == 0), stop=(q == TILES - 1))
                            last.then_inc(t_S, 1)

                        over_groups(pe, step)

                for s in layer_sems:
                    nc.sync.sem_clear(s)
                nc.all_engine_barrier()

            u_in = [sem(f"{L}in{b}") for b in range(2)]
            u_st = [sem(f"{L}st{b}") for b in range(2)]
            (u_v, u_k, u_h, u_sq, u_n, u_ho, u_row, u_H, u_V, u_N, u_y, u_yc, u_sy, u_sd, u_m, u_s) = \
                [sem(f"{L}{i}") for i in range(16)]
            loads = 1 if layer == 0 else 2
            stores = 2 if layer == 0 else 1
            with nc.Block() as block:
                @block.sync
                def _(sp):
                    for c in range(CHUNKS + 1):
                        if c < CHUNKS:
                            b = c % 2
                            if c >= 2:
                                sp.wait_ge(u_H, c - 1)
                                if layer == 1:
                                    sp.wait_ge(u_y, c - 1)
                            sp.dma_start(kst[D:2 * D, b, :], frmT[c]).then_inc(u_in[b], 16)
                            if layer == 1:
                                sp.dma_start(x1c_b[:, b, :], x1T[c]).then_inc(u_in[b], 16)
                        if c >= 1:
                            k = c - 1
                            if layer == 0:
                                sp.wait_ge(u_ho, k + 1)
                                sp.dma_start(h1T[k], ho_b[:, k % 2, :]).then_inc(u_st[k % 2], 16)
                            sp.wait_ge(u_row, k + 1)
                            sp.dma_start((h1_c, out_c)[layer][k], rows[:, k % 2, :]).then_inc(u_st[k % 2], 16)
                    sp.wait_ge(u_st[0], 16 * stores * ((CHUNKS + 1) // 2))
                    sp.wait_ge(u_st[1], 16 * stores * (CHUNKS // 2))

                @block.vector
                def _(dve):
                    v = [0]

                    def link(ins):
                        v[0] += 1
                        ins.then_inc(u_v, 1)
                        dve.wait_ge(u_v, v[0])

                    for c in range(CHUNKS):
                        b = c % 2
                        if c >= 2:
                            dve.wait_ge(u_H, c - 1)
                        dve.tensor_tensor(cols(kst[0:D, b, :]), by_slot(acc[0:D, :], c), by_slot(cnt, c), ALU.mult).then_inc(u_k, 1)
                        dve.wait_ge(u_n, c + 1)
                        link(dve.tensor_scalar(n_b[:, b, :], n_b[:, b, :], EPS_NORM, None, ALU.max))
                        link(dve.reciprocal(n_b[:, b, :], n_b[:, b, :]))
                        dve.wait_ge(u_h, c + 1)
                        if c >= 2 and layer == 0:
                            dve.wait_ge(u_N, c - 1)
                            dve.wait_ge(u_st[b], 16 * stores * (c // 2))
                        dve.scalar_tensor_tensor(out=ho_b[:, b, :], in0=h_b[:, b, :], scalar=0.0, in1=n_b[:, b, :],
                                                 op0=ALU.max, op1=ALU.mult).then_inc(u_ho, 1)
                        if layer == 1:
                            dve.wait_ge(u_ho, c + 1)
                            dve.wait_ge(u_in[b], 32 * (c // 2 + 1))
                            if c >= 2:
                                dve.wait_ge(u_N, c - 1)
                            dve.tensor_tensor(yy_b[:, b, :], ho_b[:, b, :], x1c_b[:, b, :], ALU.add).then_inc(u_y, 1)
                            dve.wait_ge(u_m, 2 * c + 1)
                            dve.tensor_tensor(ho_b[:, b, :], yy_b[:, b, :], bank[3][0:D, 0:CH], ALU.subtract).then_inc(u_yc, 1)
                            dve.wait_ge(u_sd, c + 1)
                            link(dve.reciprocal(hs_b[:, b, :], hs_b[:, b, :]))
                            dve.tensor_tensor(yy_b[:, b, :], ho_b[:, b, :], hs_b[:, b, :], ALU.mult).then_inc(u_sy, 1)
                    if layer == 0:
                        dve.memset(acc[0:D, :], 0.0)
                        dve.tensor_copy(rel[:, :, :], rel0[:, :, :])
                        dve.tensor_copy(base[:, :], base0[:, :])

                @block.scalar
                def _(act):
                    for c in range(CHUNKS):
                        b = c % 2
                        act.wait_ge(u_H, c + 1)
                        if c >= 2:
                            act.wait_ge(u_ho, c - 1)
                        act.activation(h_b[:, b, :], bank[0][0:D, 0:CH], ACT.Identity, bias=blcol[:, layer:layer + 1]).then_inc(u_h, 1)
                        act.wait_ge(u_h, c + 1)
                        if c >= 2:
                            act.wait_ge(u_V, c - 1)
                            if layer == 1:
                                act.wait_ge(u_sy, c - 1)
                        act.activation(hs_b[:, b, :], h_b[:, b, :], ACT.Square).then_inc(u_sq, 1)
                        act.wait_ge(u_V, c + 1)
                        act.activation(n_b[:, b, :], bank[1][0:D, 0:CH], ACT.Sqrt).then_inc(u_n, 1)
                        if layer == 1:
                            act.wait_ge(u_yc, c + 1)
                            act.activation(hs_b[:, b, :], ho_b[:, b, :], ACT.Square).then_inc(u_s, 1)
                            act.wait_ge(u_m, 2 * c + 2)
                            act.activation(hs_b[:, b, :], bank[4][0:D, 0:CH], ACT.Sqrt, bias=eps[0:D, 0:1]).then_inc(u_sd, 1)
                        act.wait_ge(u_N, c + 1)
                        if c >= 2:
                            act.wait_ge(u_st[b], 16 * stores * (c // 2))
                        act.copy(rows[:, b, :], bank[2][0:CP, 0:CQ * D]).then_inc(u_row, 1)

                @block.tensor
                def _(pe):
                    for c in range(CHUNKS):
                        b = c % 2
                        pe.wait_ge(u_in[b], 16 * loads * (c // 2 + 1))
                        pe.wait_ge(u_k, c + 1)
                        if c >= 1:
                            pe.wait_ge(u_h, c)
                        pe.matmul(bank[0][0:D, 0:CH], wlrT[:, layer, :], kst[:, b, :], start=True, stop=True).then_inc(u_H, 1)
                        pe.wait_ge(u_sq, c + 1)
                        pe.matmul(bank[1][0:D, 0:CH], ones[0:D, :], hs_b[:, b, :], start=True, stop=True).then_inc(u_V, 1)
                        if layer == 0:
                            pe.wait_ge(u_ho, c + 1)
                            final_b = ho_b
                        else:
                            pe.wait_ge(u_y, c + 1)
                            pe.matmul(bank[3][0:D, 0:CH], mean[:, :], yy_b[:, b, :], start=True, stop=True).then_inc(u_m, 1)
                            pe.wait_ge(u_s, c + 1)
                            pe.matmul(bank[4][0:D, 0:CH], mean[:, :], hs_b[:, b, :], start=True, stop=True).then_inc(u_m, 1)
                            pe.wait_ge(u_sy, c + 1)
                            final_b = yy_b
                        if c >= 1:
                            pe.wait_ge(u_row, c)
                        for q in range(CQ):
                            last = pe.transpose(bank[2][0:CP, q * D:(q + 1) * D], final_b[:, b, q * CP:(q + 1) * CP],
                                                ident[0:D, 0:D])
                        last.then_inc(u_N, 1)


_INS = ['x', 'src', 'dst', 'edge_attr_32', 'L0_gnn_W1f', 'L0_gnn_b1f', 'L0_gnn_W2f', 'L0_gnn_b2f',
        'L0_gnn_W1p', 'L0_gnn_b1p', 'L0_gnn_W2p', 'L0_gnn_b2p', 'L0_gnn_Wc1', 'L0_gnn_bc1', 'L0_gnn_Wc2', 'L0_gnn_bc2',
        'L1_gnn_Wl0', 'L1_gnn_bl0', 'L1_gnn_Wr0', 'L1_gnn_Wl1', 'L1_gnn_bl1', 'L1_gnn_Wr1']
_OUTS = [((N, D), 'float32')]


def kernel(**inputs):
    import numpy as _np
    import concourse.bacc as _bacc
    from concourse import mybir as _mybir
    from concourse.bass_utils import run_bass_kernel_spmd as _run

    nc = _bacc.Bacc("TRN2", target_bir_lowering=False, num_devices=1)
    arrays, args = {}, []
    for name in _INS:
        a = _np.ascontiguousarray(inputs[name])
        arrays[f"in_{name}_dram"] = a
        args.append(nc.dram_tensor(f"in_{name}_dram", a.shape, _mybir.dt.from_np(a.dtype), kind="ExternalInput").ap())
    for i, (shape, dtype) in enumerate(_OUTS):
        dt = _mybir.dt.from_np(_np.dtype(dtype))
        args.append(nc.dram_tensor(f"out_{i}_dram", shape, dt, kind="ExternalOutput").ap())
    build(nc, *args)
    r = _run(nc, [arrays], core_ids=[0])
    return r.results[0]["out_0_dram"]
```

```python
from contextlib import ExitStack

import concourse.bass as bass
from concourse import mybir

F32 = mybir.dt.float32
I32 = mybir.dt.int32
ALU = mybir.AluOpType
ACT = mybir.ActivationFunctionType
AX_X = mybir.AxisListType.X

P = 128
N = 12500
E = 200000
D = 64
DE = 32
H = 128
TILES = 4
GROUP = TILES * P
GROUPS = -(-E // GROUP)
LAST = E - GROUP
OVERLAP = (GROUPS - 1) * GROUP - LAST
PAIRS = (GROUPS - 1) // 2
W = 64
NW = N + W
CH = 500
CP, CQ = 125, 4
CHUNKS = N // CH
NB = 3
WEIGHTS = 19
ROWS = 12800
ZCOLS = ROWS * D // P
LOADS = [98, 98, 98, GROUPS - 3 * 98]
EPS_LN = 1e-5
EPS_NORM = 1e-12
SLOPE = 0.01


def build(nc, x, src, dst, ea, W1f, b1f, W2f, b2f, W1p, b1p, W2p, b2p, Wc1, bc1, Wc2, bc2,
          Wl0, bl0, Wr0, Wl1, bl1, Wr1, out):
    Ap = nc.dram_tensor("Ap", [N, H], F32).ap()
    Af = nc.dram_tensor("Af", [NW, H], F32).ap()
    future = [nc.dram_tensor(f"future{q}", [ROWS, D], F32).ap() for q in range(TILES)]
    xT = nc.dram_tensor("xT", [CHUNKS, D, CH], F32).ap()
    x1T = nc.dram_tensor("x1T", [CHUNKS, D, CH], F32).ap()
    h1T = nc.dram_tensor("h1T", [CHUNKS, D, CH], F32).ap()
    x1 = nc.dram_tensor("x1", [N, D], F32).ap()
    h1 = nc.dram_tensor("h1", [N, D], F32).ap()

    ctx = ExitStack()
    with ctx:
        def sb(name, shape, dt=F32):
            return ctx.enter_context(nc.sbuf_tensor(name, shape, dt))

        stage = [ExitStack()]

        def tmp(name, shape, dt=F32):
            return stage[0].enter_context(nc.sbuf_tensor(name, shape, dt))

        stage_sems = []

        def tsem(name):
            stage_sems.append(stage[0].enter_context(nc.semaphore(name)))
            return stage_sems[-1]

        def clear(sems):
            for s in sems:
                nc.sync.sem_clear(s)
            nc.all_engine_barrier()

        def next_stage():
            if stage_sems:
                clear(stage_sems)
            stage_sems.clear()
            stage[0].close()
            stage[0] = ExitStack()

        def ps(name, shape):
            return ctx.enter_context(nc.psum_tensor(name, shape, F32))

        def sem(name):
            return ctx.enter_context(nc.semaphore(name))

        bank = [ps(f"bank{i}", [P, 512]) for i in range(8)]

        acc = sb("acc", [P, NW])
        cnt = sb("cnt", [D, NW])

        ident = sb("ident", [P, P])
        centre2 = sb("centre2", [D, D])
        triu = sb("triu", [P, P])
        ones = sb("ones", [P, D])
        mean = sb("mean", [D, D])
        window = sb("window", [P, W])
        window_i = sb("window_i", [P, W], I32)
        dump = sb("dump", [P, 1])
        dump_i = sb("dump_i", [P, 1], I32)
        eps = sb("eps", [P, 1])

        w1x = sb("w1x", [D + 1, 2 * H])
        w1pe = sb("w1pe", [DE, H])
        w2f = sb("w2f", [H, D])
        w2p = sb("w2p", [H, D])
        b2frow = sb("b2frow", [P, D])
        b2pcol = sb("b2pcol", [D, 1])
        wc1 = sb("wc1", [2 * D, H])
        bc1col = sb("bc1col", [H, 1])
        wc2 = sb("wc2", [H, D])
        bc2col = sb("bc2col", [D, 1])
        wc2c = sb("wc2c", [H, D])
        bc2c = sb("bc2c", [D, 1])
        wlr = sb("wlr", [D, 2, 2 * D])
        wlrT = sb("wlrT", [2 * D, 2, D])
        blcol = sb("blcol", [D, 2])

        src_i = sb("src_i", [P, GROUPS, TILES], I32)
        rel0 = sb("rel0", [P, GROUPS, TILES])
        rel = sb("rel", [P, GROUPS, TILES])
        base0 = sb("base0", [1, GROUPS])
        base = sb("base", [1, GROUPS])
        base_i = sb("base_i", [1, GROUPS], I32)
        gidx = sb("gidx", [P, 2, TILES], I32)
        rounds_i = sb("rounds_i", [1, 1], I32)

        s_const = sem("s_const")
        s_weights = sem("s_weights")
        s_iota = sem("s_iota")

        def weight_loads(sp):
            loads = [
                (w1x[0:D, 0:H], W1p[0:D, :]), (w1x[0:D, H:2 * H], W1f[0:D, :]),
                (w1x[D:D + 1, 0:H], b1p.rearrange("(a n) -> a n", a=1)),
                (w1x[D:D + 1, H:2 * H], b1f.rearrange("(a n) -> a n", a=1)),
                (w1pe[:, :], W1p[D:D + DE, :]),
                (w2f[:, :], W2f), (w2p[:, :], W2p),
                (b2frow[:, :], b2f.rearrange("(a n) -> a n", a=1).to_broadcast([P, D])),
                (b2pcol[:, :], b2p.rearrange("(n a) -> n a", a=1)),
                (wc1[:, :], Wc1),
                (bc1col[:, :], bc1.rearrange("(n a) -> n a", a=1)),
                (wc2[:, :], Wc2), (bc2col[:, :], bc2.rearrange("(n a) -> n a", a=1)),
                (wlr[:, 0, 0:D], Wl0), (wlr[:, 0, D:2 * D], Wr0),
                (wlr[:, 1, 0:D], Wl1), (wlr[:, 1, D:2 * D], Wr1),
                (blcol[:, 0:1], bl0.rearrange("(n a) -> n a", a=1)),
                (blcol[:, 1:2], bl1.rearrange("(n a) -> n a", a=1)),
            ]
            for to, frm in loads:
                sp.dma_start(to, frm).then_inc(s_weights, 16)
            assert len(loads) == WEIGHTS

        def natural(t):
            return t.rearrange("k (p q) -> k q p", q=CQ)

        def slots(t):
            return t.rearrange("k (q p) -> k q p", q=CQ)

        src_g = tmp("src_g", [98, 4, GROUP], I32)
        dst_g = tmp("dst_g", [98, 4, GROUP], I32)
        src_f = src_g[:, :, :].bitcast(F32)
        dst_f = dst_g[:, :, :].bitcast(F32)
        low = tmp("low", [98, 4])
        high = tmp("high", [98, 4])
        span = tmp("span", [98, 4])
        spans = tmp("spans", [1, GROUPS])
        widest = tmp("widest", [1, 1])
        widest_i = tmp("widest_i", [1, 1], I32)
        more_i = tmp("more_i", [1, 1], I32)
        lastrows = LOADS[3]
        parts = [(0, 98, 0, 3), (0, lastrows, 3, 4)]
        zero = tmp("zero", [P, ZCOLS // 2])
        xin = tmp("xin", [CP, NB, CQ * D])
        chunkT = tmp("chunkT", [D + 1, NB, CH])
        table = tmp("table", [CP, NB, CQ, 2 * H])
        centre = tmp("centre", [D, D])
        wc2T = tmp("wc2T", [D, H])
        x_c = x.rearrange("(c p q) d -> c p (q d)", p=CP, q=CQ)
        Ap_c = Ap.rearrange("(c p q) h -> c p q h", p=CP, q=CQ)
        Af_c = Af[0:N, :].rearrange("(c p q) h -> c p q h", p=CP, q=CQ)

        (s_float, s_ext, s_rel, s_turn, s_turned, s_rowt, s_row, s_clear, s_centre, s_wt, s_wtc, s_wc,
         sA_zero, sA_t, sA_T, sA_h, sA_evac, sA_evad, sA_ones) = [tsem(f"set{i}") for i in range(19)]
        sA_zeroed = sem("sA_zeroed")
        s_idx = [tsem(f"s_idx{i}") for i in range(2)]
        sA_x = [tsem(f"sA_x{b}") for b in range(NB)]
        sA_xT = [sem(f"sA_xT{b}") for b in range(NB)]
        sA_store = [sem(f"sA_store{b}") for b in range(NB)]
        with nc.Block() as block:
            @block.sync
            def _(sp):
                def load_x(c):
                    if c >= NB:
                        sp.wait_ge(sA_t, c - NB + 1)
                    sp.dma_start(xin[:, c % NB, :], x_c[c]).then_inc(sA_x[c % NB], 16)

                load_x(0)
                for k, (a, to) in enumerate(((dst, dst_g), (src, src_g))):
                    g0 = 0
                    for c, size in enumerate(LOADS):
                        full = size - (c == 3)
                        sp.dma_start(to[0:full, c, :], a[g0 * GROUP:(g0 + full) * GROUP].rearrange(
                            "(g e) -> g e", e=GROUP)).then_inc(s_idx[k], 16)
                        g0 += size
                    sp.dma_start(to[lastrows - 1:lastrows, 3, :],
                                 a[LAST:E].rearrange("(g e) -> g e", e=GROUP)).then_inc(s_idx[k], 16)
                    if k == 0:
                        weight_loads(sp)
                for c in range(1, CHUNKS):
                    load_x(c)

            @block.gpsimd
            def _(pool):
                nc.gpsimd.memset(ident[:, :], 0.0).then_inc(s_iota, 1)
                nc.gpsimd.memset(triu[:, :], 1.0).then_inc(s_iota, 1)
                nc.gpsimd.memset(ones[:, :], 1.0).then_inc(s_const, 1)
                nc.gpsimd.memset(mean[:, :], 1.0 / D).then_inc(s_const, 1)
                nc.gpsimd.memset(eps[:, :], EPS_LN).then_inc(s_const, 1)
                nc.gpsimd.iota(window_i[:, :], pattern=[[1, W]], base=0, channel_multiplier=0).then_inc(s_iota, 1)
                nc.gpsimd.iota(dump_i[:, :], pattern=[[0, 1]], base=N, channel_multiplier=1).then_inc(s_iota, 1)
                pool.wait_ge(s_iota, 4)
                nc.gpsimd.affine_select(out=ident[:, :], in_=ident[:, :], compare_op=ALU.not_equal, fill=1.0,
                                        base=0, pattern=[[-1, P]], channel_multiplier=1).then_inc(s_const, 1)
                nc.gpsimd.memset(zero[:, :], 0.0).then_inc(sA_zero, 1)
                nc.gpsimd.affine_select(out=triu[:, :], in_=triu[:, :], compare_op=ALU.is_ge, fill=0.0,
                                        base=0, pattern=[[1, P]], channel_multiplier=-1).then_inc(s_const, 1)
                nc.gpsimd.tensor_copy(window[:, :], window_i[:, :]).then_inc(s_const, 1)
                nc.gpsimd.tensor_copy(dump[:, :], dump_i[:, :]).then_inc(s_const, 1)
                pool.wait_ge(sA_zero, 1)
                for q in range(TILES):
                    half = future[q].rearrange("(h p r) d -> h p (r d)", h=2, p=P)
                    for h in range(2):
                        pool.dma_start(half[h], zero[:, :]).then_inc(sA_zeroed, 16)
                pool.dma_start(Af[N:NW, :], zero[0:W, 0:H]).then_inc(sA_zeroed, 16)
                nc.gpsimd.memset(acc[:, :], 0.0).then_inc(s_clear, 1)
                nc.gpsimd.memset(cnt[:, :], 0.0).then_inc(s_clear, 1)
                for c in range(CHUNKS):
                    b = c % NB
                    pool.wait_ge(sA_T, c + 1)
                    pool.dma_start(xT[c], chunkT[0:D, b, :]).then_inc(sA_xT[b], 16)
                    pool.wait_ge(sA_evac, c + 1)
                    pool.wait_ge(sA_evad, c + 1)
                    pool.dma_start(Ap_c[c], table[:, b, :, 0:H]).then_inc(sA_store[b], 16)
                    pool.dma_start(Af_c[c], table[:, b, :, H:2 * H]).then_inc(sA_store[b], 16)
                pool.wait_ge(sA_zeroed, 16 * (2 * TILES + 1))
                for b in range(NB):
                    n = len(range(b, CHUNKS, NB))
                    pool.wait_ge(sA_store[b], 32 * n)
                    pool.wait_ge(sA_xT[b], 16 * n)

            @block.scalar
            def _(act):
                for t in range(CHUNKS + 1):
                    if t >= 1:
                        c = t - 1
                        if c >= NB:
                            act.wait_ge(sA_store[c % NB], 32 * (c // NB))
                        act.wait_ge(sA_h, c + 1)
                        act.copy(table[:, c % NB, 0:2, :], bank[2 + 2 * (c % 2)][0:CP, :].rearrange(
                            "p (q n) -> p q n", q=2)).then_inc(sA_evac, 1)
                    if t < CHUNKS:
                        if t >= NB:
                            act.wait_ge(sA_h, t - NB + 1)
                            act.wait_ge(sA_xT[t % NB], 16 * (t // NB))
                        act.wait_ge(sA_t, t + 1)
                        act.copy(natural(chunkT[0:D, t % NB, :]), slots(bank[t % 2][0:D, 0:CH])).then_inc(sA_T, 1)

            @block.tensor
            def _(pe):
                pe.wait_ge(s_const, 7)
                pe.wait_ge(sA_ones, 1)
                pe.wait_ge(s_weights, 16 * WEIGHTS)
                for l in range(2):
                    pe.transpose(bank[6][:, l * D:(l + 1) * D], wlr[:, l, :], ident[0:D, 0:D])
                pe.transpose(bank[6][0:D, H:2 * H], wc2[:, :], ident[:, :]).then_inc(s_wt, 1)
                for t in range(CHUNKS + 1):
                    if t < CHUNKS:
                        pe.wait_ge(sA_x[t % NB], 16 * (t // NB + 1))
                        if t >= 2:
                            pe.wait_ge(sA_T, t - 1)
                        for q in range(CQ):
                            last = pe.transpose(bank[t % 2][0:D, q * CP:(q + 1) * CP],
                                                xin[:, t % NB, q * D:(q + 1) * D], ident[0:CP, 0:CP])
                        last.then_inc(sA_t, 1)
                    if t >= 1:
                        c = t - 1
                        pe.wait_ge(sA_T, c + 1)
                        if c >= 2:
                            pe.wait_ge(sA_evac, c - 1)
                            pe.wait_ge(sA_evad, c - 1)
                        v = natural(chunkT[:, c % NB, :])
                        for q in range(CQ):
                            last = pe.matmul(bank[2 + 2 * (c % 2) + q // 2][0:CP, (q % 2) * 256:(q % 2) * 256 + 256],
                                             v[:, q, :], w1x[:, :], start=True, stop=True)
                        last.then_inc(sA_h, 1)
                pe.wait_ge(s_wtc, 2)
                pe.wait_ge(s_centre, 2)
                pe.matmul(bank[7][:, 0:D], wc2T[:, :], centre[:, :], start=True, stop=True)
                pe.matmul(bank[7][0:D, D:D + 1], centre[:, :], bc2col[:, :], start=True, stop=True).then_inc(s_wc, 1)
                pe.wait_ge(s_rel, 6)
                k = 0
                for c, size in enumerate(LOADS):
                    for frm in (dst_f, src_f):
                        if k >= 2:
                            pe.wait_ge(s_turned, k - 1)
                        v = frm[0:size, c, :].rearrange("g (p q) -> g q p", q=TILES)
                        for q in range(TILES):
                            last = pe.transpose(bank[k % 2][:, q * size:(q + 1) * size], v[:, q, :],
                                                ident[0:size, 0:size])
                        last.then_inc(s_turn, 1)
                        k += 1
                pe.wait_ge(sA_evac, CHUNKS)
                pe.wait_ge(sA_evad, CHUNKS)
                g0 = 0
                for c, size in enumerate(LOADS):
                    pe.transpose(bank[2][0:1, g0:g0 + size], low[0:size, c:c + 1], ident[0:size, 0:size])
                    last = pe.transpose(bank[3][0:1, g0:g0 + size], span[0:size, c:c + 1], ident[0:size, 0:size])
                    g0 += size
                last.then_inc(s_rowt, 1)

            @block.vector
            def _(dve):
                def table_half(c):
                    if c >= NB:
                        dve.wait_ge(sA_store[c % NB], 32 * (c // NB))
                    dve.wait_ge(sA_h, c + 1)
                    dve.tensor_copy(table[:, c % NB, 2:4, :], bank[3 + 2 * (c % 2)][0:CP, :].rearrange(
                        "p (q n) -> p q n", q=2)).then_inc(sA_evad, 1)

                dve.memset(chunkT[D:D + 1, :, :], 1.0).then_inc(sA_ones, 1)
                dve.wait_ge(s_idx[0], 16 * 5)
                for p0, p1, c0, c1 in parts:
                    dve.tensor_copy(dst_f[p0:p1, c0:c1, :], dst_g[p0:p1, c0:c1, :]).then_inc(s_float, 1)
                table_half(0)
                dve.wait_ge(s_float, 2)
                for p0, p1, c0, c1 in parts:
                    dve.tensor_reduce(low[p0:p1, c0:c1], dst_f[p0:p1, c0:c1, :], AX_X, ALU.min).then_inc(s_ext, 1)
                    dve.tensor_reduce(high[p0:p1, c0:c1], dst_f[p0:p1, c0:c1, :], AX_X, ALU.max).then_inc(s_ext, 1)
                table_half(1)
                dve.wait_ge(s_ext, 4)
                for c in range(4):
                    dve.tensor_scalar(dst_f[0:LOADS[c], c, :], dst_f[0:LOADS[c], c, :], low[0:LOADS[c], c:c + 1],
                                      None, ALU.subtract).then_inc(s_rel, 1)
                for p0, p1, c0, c1 in parts:
                    dve.tensor_tensor(span[p0:p1, c0:c1], high[p0:p1, c0:c1], low[p0:p1, c0:c1],
                                      ALU.subtract).then_inc(s_rel, 1)
                table_half(2)
                dve.wait_ge(s_idx[1], 16 * 5)
                for p0, p1, c0, c1 in parts:
                    dve.tensor_copy(src_f[p0:p1, c0:c1, :], src_g[p0:p1, c0:c1, :]).then_inc(s_float, 1)
                dve.wait_ge(s_float, 4)
                dve.wait_ge(s_wt, 1)
                dve.tensor_copy(wlrT[:, :, :], bank[6][:, 0:2 * D].rearrange("p (l d) -> p l d", l=2)).then_inc(s_wtc, 1)
                dve.tensor_copy(wc2T[:, :], bank[6][0:D, H:2 * H]).then_inc(s_wtc, 1)
                dve.wait_ge(s_const, 7)
                dve.tensor_tensor(centre[:, :], ident[0:D, 0:D], mean[:, :], ALU.subtract).then_inc(s_centre, 1)
                dve.wait_ge(s_centre, 1)
                dve.tensor_scalar(centre2[:, :], centre[:, :], 2.0, None, ALU.mult).then_inc(s_centre, 1)
                for c in range(3, CHUNKS):
                    table_half(c)
                dve.wait_ge(s_wc, 1)
                dve.tensor_copy(wc2c[:, :], bank[7][:, 0:D])
                dve.tensor_copy(bc2c[:, :], bank[7][0:D, D:D + 1])
                k = 0
                g0 = 0
                for c, size in enumerate(LOADS):
                    for to in (rel0, src_i):
                        dve.wait_ge(s_turn, k + 1)
                        t = bank[k % 2][:, 0:TILES * size].rearrange("p (q g) -> p q g", q=TILES)
                        dve.tensor_copy(to[:, g0:g0 + size, :].rearrange("p g q -> p q g"), t).then_inc(s_turned, 1)
                        k += 1
                    g0 += size
                dve.wait_ge(s_turned, 8)
                dve.memset(rel0[0:OVERLAP // TILES, GROUPS - 1, :], -1.0e6).then_inc(s_turned, 1)
                dve.wait_ge(s_rowt, 1)
                dve.tensor_copy(base0[:, :], bank[2][0:1, 0:GROUPS]).then_inc(s_turned, 1)
                dve.tensor_copy(spans[:, :], bank[3][0:1, 0:GROUPS]).then_inc(s_row, 1)
                dve.wait_ge(s_row, 1)
                dve.tensor_reduce(widest[:, :], spans[:, :], AX_X, ALU.max).then_inc(s_row, 1)
                dve.wait_ge(s_row, 2)
                dve.tensor_copy(widest_i[:, :], widest[:, :]).then_inc(s_row, 1)
                dve.wait_ge(s_row, 3)
                dve.tensor_single_scalar(more_i[:, :], widest_i[:, :], W.bit_length() - 1, ALU.logical_shift_right).then_inc(s_row, 1)
                dve.wait_ge(s_row, 4)
                dve.tensor_scalar(rounds_i[:, :], more_i[:, :], 1, None, ALU.add).then_inc(s_row, 1)
                dve.wait_ge(s_turned, 10)
                dve.tensor_copy(rel[:, :, :], rel0[:, :, :])
                dve.tensor_copy(base[:, :], base0[:, :])

        next_stage()

        rounds = nc.values_load(rounds_i[0:1, 0:1], min_val=1, max_val=N // W + 1)

        srcm = tmp("srcm", [P, GROUPS, TILES])
        inwin = tmp("inwin", [P, GROUPS, TILES])
        comb = tmp("comb", [P, 2, TILES, DE + W])
        wwin = tmp("wwin", [DE + W, 2, H])
        gbuf = tmp("gbuf", [P, 2, TILES, H])
        skey = tmp("skey", [P, 2, TILES])
        equal = tmp("equal", [P, 2, TILES, P])
        later = tmp("later", [P, 2, TILES])
        away = tmp("away", [P, 2, TILES])
        pick = tmp("pick", [P, 2, TILES])
        sidx = tmp("sidx", [P, 2, TILES], I32)
        featT = tmp("featT", [DE + W, 2, GROUP])
        hidf = tmp("hidf", [H, 2, GROUP])
        msg = tmp("msg", [P, 2, TILES, D])
        sbuf = tmp("sbuf", [P, 2, TILES, D])
        pre = tmp("pre", [P, 2, GROUP])
        hidp = tmp("hidp", [P, 2, GROUP])

        psR, psT, psF, psP, psM, psD, psS = bank[0:7]

        edge_sems = []

        def esem(name):
            edge_sems.append(stage[0].enter_context(nc.semaphore(name)))
            return edge_sems[-1]

        s_prep = esem("s_prep")
        s_wedge = esem("s_wedge")
        s_ea = [esem(f"s_ea{b}") for b in range(2)]
        s_win = [esem(f"s_win{b}") for b in range(2)]
        s_gat = [sem(f"s_gat{b}") for b in range(2)]
        s_sc = [sem(f"s_sc{q}") for q in range(TILES)]
        gathered = [16 * TILES * (PAIRS + 1), 16 * TILES * PAIRS]
        added = 16 * GROUPS
        s_open = esem("s_open")
        s_scdone = esem("s_scdone")
        s_gidx = esem("s_gidx")
        s_sm = esem("s_sm")
        s_oh = esem("s_oh")
        s_eu = esem("s_eu")
        s_away = esem("s_away")
        s_pick = esem("s_pick")
        s_sidx = esem("s_sidx")
        s_msb = esem("s_msb")
        s_pre = esem("s_pre")
        s_acc = esem("s_acc")
        s_stk = esem("s_stk")
        s_slope = esem("s_slope")
        s_hf = esem("s_hf")
        s_hp = esem("s_hp")
        s_sb = esem("s_sb")
        s_R = esem("s_R")
        s_T = esem("s_T")
        s_F = esem("s_F")
        s_P = esem("s_P")
        s_M = esem("s_M")
        s_D = esem("s_D")
        s_S = esem("s_S")

        def over_groups(eng, step, first=0):
            step(0, 0, 0, True)
            step(1, 0, 1, True)
            with eng.Fori(1, PAIRS) as i:
                step(2 * i, i, 0, False)
                step(2 * i + 1, i, 1, False)
            step(GROUPS - 1, PAIRS, 0, False)

        def final(g):
            return isinstance(g, int) and g == GROUPS - 1

        def windows(dve, done):
            dve.tensor_scalar(base_i[:, :], base[:, :], float(N), None, ALU.min).then_inc(done, 1)

        def next_windows(dve):
            dve.tensor_scalar(rel[:, :, :], rel[:, :, :], -float(W), None, ALU.add)
            dve.tensor_scalar(base[:, :], base[:, :], float(W), None, ALU.add)

        ea_main = ea[0:(GROUPS - 1) * GROUP, :].rearrange("(g p q) f -> g p q f", p=P, q=TILES)
        ea_last = ea[LAST:E, :].rearrange("(p q) f -> p q f", q=TILES)
        window_b = window[:, :].unsqueeze(1).to_broadcast([P, TILES, W])

        with nc.Fori(0, rounds) as r:
            with nc.Block() as block:
                @block.sync
                def _(sp):
                    for b in range(2):
                        sp.dma_start(wwin[0:DE, b, :], W1f[D:D + DE, :]).then_inc(s_wedge, 16)
                    sp.wait_ge(s_prep, 4)

                    def step(g, pair, b, early):
                        if not early:
                            sp.wait_ge(s_T, g - 1)
                        sp.dma_start(comb[:, b, :, 0:DE], ea_last if final(g) else ea_main[g]).then_inc(s_ea[b], 16)
                        row = sp.value_load(base_i[0:1, g:g + 1] if isinstance(g, int)
                                            else base_i[0:1, bass.DynSlice(g, 1)], min_val=0, max_val=N)
                        if not early:
                            sp.wait_ge(s_F, g - 1)
                        sp.dma_start(wwin[DE:DE + W, b, :], Af[bass.DynSlice(row, W), :]).then_inc(s_win[b], 16)

                    over_groups(sp, step)

                @block.gpsimd
                def _(pool):
                    def gathers(b):
                        for q in range(TILES):
                            pool.indirect_dma_start(
                                out=gbuf[:, b, q, :], out_offset=None, in_=Ap[:, :],
                                in_offset=bass.IndirectOffsetOnAxis(ap=gidx[:, b, q:q + 1], axis=0)).then_inc(s_gat[b], 16)

                    pool.wait_ge(s_gidx, 1)
                    gathers(0)

                    def step(g, pair, b, early):
                        if not final(g):
                            if not (isinstance(g, int) and g == 0):
                                pool.wait_ge(s_pre, g)
                            pool.wait_ge(s_gidx, g + 2)
                            pool.sem_inc(s_open, 1)
                            gathers(1 - b)
                        if not (isinstance(g, int) and g == 0):
                            for q in range(TILES):
                                pool.wait_ge(s_sc[q], r * added + 16 * g)
                        pool.wait_ge(s_sidx, g + 1)
                        pool.wait_ge(s_sb, g + 1)
                        pool.sem_inc(s_scdone, 1)
                        for q in range(TILES):
                            pool.indirect_dma_start(
                                out=future[q][:, :],
                                out_offset=bass.IndirectOffsetOnAxis(ap=sidx[:, b, q:q + 1], axis=0),
                                in_=sbuf[:, b, q, :], in_offset=None, compute_op=ALU.add).then_inc(s_sc[q], 16)

                    over_groups(pool, step)
                    for q in range(TILES):
                        pool.wait_ge(s_sc[q], r * added + added)

                @block.vector
                def _(dve):
                    windows(dve, s_prep)
                    dve.tensor_single_scalar(inwin[:, :, :], rel[:, :, :], 0.0, ALU.is_ge).then_inc(s_prep, 1)
                    dve.tensor_scalar(srcm[:, :, :], src_i[:, :, :], dump[:, 0:1], None, ALU.subtract).then_inc(s_prep, 1)
                    dve.wait_ge(s_prep, 3)
                    dve.scalar_tensor_tensor(out=inwin[:, :, :], in0=rel[:, :, :], scalar=float(W), in1=inwin[:, :, :],
                                             op0=ALU.is_lt, op1=ALU.mult).then_inc(s_prep, 1)
                    dve.wait_ge(s_prep, 4)
                    dve.tensor_tensor(srcm[:, :, :], srcm[:, :, :], inwin[:, :, :], ALU.mult).then_inc(s_prep, 1)
                    dve.wait_ge(s_prep, 5)
                    dve.tensor_scalar(srcm[:, :, :], srcm[:, :, :], dump[:, 0:1], None, ALU.add).then_inc(s_prep, 1)
                    dve.tensor_copy(gidx[:, 0, :], src_i[:, 0, :]).then_inc(s_gidx, 1)
                    dve.wait_ge(s_prep, 6)

                    def col(t, g):
                        return t[:, g, :] if isinstance(g, int) else t[:, bass.DynSlice(g, 1), :].rearrange("p a q -> p (a q)")

                    def add_sums(g):
                        at = dve.value_load(base_i[0:1, g:g + 1] if isinstance(g, int)
                                            else base_i[0:1, bass.DynSlice(g, 1)], min_val=0, max_val=N)
                        if not (isinstance(g, int) and g == 0):
                            dve.wait_ge(s_acc, 2 * g)
                        dve.wait_ge(s_S, g + 1)
                        v = acc[:, bass.DynSlice(at, W)]
                        dve.tensor_tensor(v, v, psS[:, 0:W], ALU.add).then_inc(s_acc, 1)
                        v = cnt[:, bass.DynSlice(at, W)]
                        dve.tensor_tensor(v, v, psS[0:D, W:2 * W], ALU.add).then_inc(s_acc, 1)

                    def step(g, pair, b, early):
                        if not final(g):
                            dve.tensor_copy(gidx[:, 1 - b, :], col(src_i, g + 1)).then_inc(s_gidx, 1)
                        if not early:
                            dve.wait_ge(s_R, g - 1)
                        dve.tensor_copy(skey[:, b, :], col(srcm, g)).then_inc(s_sm, 1)
                        if not early:
                            dve.wait_ge(s_S, g - 1)
                        dve.tensor_tensor(comb[:, b, :, DE:DE + W], window_b,
                                          col(rel, g).unsqueeze(2).to_broadcast([P, TILES, W]),
                                          ALU.is_equal).then_inc(s_oh, 1)
                        dve.wait_ge(s_sm, g + 1)
                        dve.tensor_scalar(away[:, b, :], skey[:, b, :], dump[:, 0:1], None, ALU.subtract).then_inc(s_away, 1)
                        if not early:
                            dve.wait_ge(s_D, g - 1)
                        dve.wait_ge(s_R, g + 1)
                        for q in range(TILES):
                            dve.scalar_tensor_tensor(out=equal[:, b, q, :], in0=psR[:, q * P:(q + 1) * P],
                                                     scalar=skey[:, b, q:q + 1], in1=triu[:, :],
                                                     op0=ALU.is_equal, op1=ALU.mult,
                                                     accum_out=later[:, b, q:q + 1]).then_inc(s_eu, 1)
                        if not (isinstance(g, int) and g == 0):
                            add_sums(g - 1)
                        dve.wait_ge(s_away, g + 1)
                        dve.wait_ge(s_eu, 4 * g + 4)
                        dve.scalar_tensor_tensor(out=pick[:, b, :], in0=later[:, b, :], scalar=1.0, in1=away[:, b, :],
                                                 op0=ALU.is_equal, op1=ALU.mult).then_inc(s_pick, 1)
                        if not early:
                            dve.wait_ge(s_scdone, g)
                        dve.wait_ge(s_pick, g + 1)
                        dve.tensor_scalar(sidx[:, b, :], pick[:, b, :], dump[:, 0:1], None, ALU.add).then_inc(s_sidx, 1)
                        dve.wait_ge(s_slope, g + 1)
                        dve.tensor_tensor(hidf[:, b, :], hidf[:, b, :], psF[:, :], ALU.max).then_inc(s_hf, 1)
                        dve.wait_ge(s_gat[b], r * gathered[b] + (64 * pair + 64))
                        dve.wait_ge(s_P, g + 1)
                        dve.tensor_tensor(pre[:, b, :], psP[:, :], gbuf[:, b, :, :].rearrange("p q h -> p (q h)"),
                                          ALU.add).then_inc(s_pre, 1)
                        dve.wait_ge(s_M, g + 1)
                        dve.tensor_tensor(msg[:, b, :, :], psM[:, 0:TILES * D].rearrange("p (q d) -> p q d", q=TILES),
                                          b2frow[:, :].unsqueeze(1).to_broadcast([P, TILES, D]),
                                          ALU.add).then_inc(s_msb, 1)
                        dve.wait_ge(s_pre, g + 1)
                        dve.scalar_tensor_tensor(out=hidp[:, b, :], in0=pre[:, b, :], scalar=SLOPE, in1=pre[:, b, :],
                                                 op0=ALU.mult, op1=ALU.max).then_inc(s_hp, 1)

                    over_groups(dve, step)
                    add_sums(GROUPS - 1)
                    next_windows(dve)

                @block.scalar
                def _(act):
                    def step(g, pair, b, early):
                        if not early:
                            act.wait_ge(s_P, g - 1)
                        act.wait_ge(s_T, g + 1)
                        act.copy(featT[:, b, :], psT[0:DE + W, :]).then_inc(s_stk, 1)
                        if not early:
                            act.wait_ge(s_M, g - 1)
                        act.wait_ge(s_F, g + 1)
                        act.activation(hidf[:, b, :], psF[:, :], ACT.Copy, scale=SLOPE).then_inc(s_slope, 1)
                        if not early:
                            act.wait_ge(s_scdone, g)
                        act.wait_ge(s_D, g + 1)
                        act.copy(sbuf[:, b, :, :], psD[:, 0:TILES * D].rearrange("p (q d) -> p q d", q=TILES)).then_inc(s_sb, 1)

                    over_groups(act, step)

                @block.tensor
                def _(pe):
                    def sums(g, b):
                        if not (isinstance(g, int) and g == 0):
                            pe.wait_ge(s_acc, 2 * g)
                        pe.wait_ge(s_hp, g + 1)
                        for q in range(TILES):
                            pe.matmul(psS[:, 0:W], hidp[:, b, q * P:(q + 1) * P], comb[:, b, q, DE:DE + W],
                                      start=(q == 0), stop=(q == TILES - 1))
                        for q in range(TILES):
                            last = pe.matmul(psS[0:D, W:2 * W], ones[:, :], comb[:, b, q, DE:DE + W],
                                             start=(q == 0), stop=(q == TILES - 1))
                        last.then_inc(s_S, 1)

                    pe.wait_ge(s_wedge, 32)

                    def step(g, pair, b, early):
                        first = isinstance(g, int) and g == 0
                        if not first:
                            pe.wait_ge(s_eu, 4 * g)
                        pe.wait_ge(s_sm, g + 1)
                        for q in range(TILES):
                            last = pe.transpose(psR[:, q * P:(q + 1) * P],
                                                skey[:, b, q:q + 1].to_broadcast([P, P]), ident[:, :])
                        last.then_inc(s_R, 1)
                        pe.wait_ge(s_ea[b], 16 * pair + 16)
                        if not first:
                            pe.wait_ge(s_stk, g)
                        pe.wait_ge(s_oh, g + 1)
                        for q in range(TILES):
                            last = pe.transpose(psT[0:DE + W, q * P:(q + 1) * P], comb[:, b, q, :], ident[:, :])
                        last.then_inc(s_T, 1)
                        if not first:
                            sums(g - 1, 1 - b)
                        pe.wait_ge(s_win[b], 16 * pair + 16)
                        if not first:
                            pe.wait_ge(s_hf, g)
                        pe.wait_ge(s_stk, g + 1)
                        pe.matmul(psF[:, :], wwin[:, b, :], featT[:, b, :], start=True, stop=True).then_inc(s_F, 1)
                        if not first:
                            pe.wait_ge(s_pre, g)
                        for q in range(TILES):
                            last = pe.matmul(psP[:, q * H:(q + 1) * H], featT[0:DE, b, q * P:(q + 1) * P], w1pe[:, :],
                                             start=True, stop=True)
                        last.then_inc(s_P, 1)
                        if not first:
                            pe.wait_ge(s_msb, g)
                        pe.wait_ge(s_hf, g + 1)
                        for q in range(TILES):
                            last = pe.matmul(psM[:, q * D:(q + 1) * D], hidf[:, b, q * P:(q + 1) * P], w2f[:, :],
                                             start=True, stop=True)
                        last.then_inc(s_M, 1)
                        if not first:
                            pe.wait_ge(s_sb, g)
                        pe.wait_ge(s_eu, 4 * g + 4)
                        pe.wait_ge(s_msb, g + 1)
                        for q in range(TILES):
                            last = pe.matmul(psD[:, q * D:(q + 1) * D], equal[:, b, q, :], msg[:, b, q, :],
                                             start=True, stop=True)
                        last.then_inc(s_D, 1)

                    over_groups(pe, step)
                    sums(GROUPS - 1, 0)

            clear(edge_sems)

        next_stage()

        def stages(*works):
            for t in range(CHUNKS + len(works) - 1):
                for s in reversed(range(len(works))):
                    if works[s] and 0 <= t - s < CHUNKS:
                        works[s](t - s)

        def buffers(where, *shapes):
            return [tmp(f"{where}_{name}", [rows, NB, n]) for name, rows, n in shapes]

        x1_c = x1.rearrange("(c p q) d -> c p (q d)", p=CP, q=CQ)
        h1_c = h1.rearrange("(c p q) d -> c p (q d)", p=CP, q=CQ)
        out_c = out.rearrange("(c p q) d -> c p (q d)", p=CP, q=CQ)
        future_c = [f[0:N, :].rearrange("(c p q) d -> c p (q d)", p=CP, q=CQ) for f in future]

        def chunk(t, c):
            return t[:, c * CH:(c + 1) * CH]

        def stored(sems, c, each=1):
            return sems[c % NB], 16 * each * (c // NB)

        def all_stored(eng, sems, each=1):
            for b in range(NB):
                eng.wait_ge(sems[b], 16 * each * len(range(b, CHUNKS, NB)))

        fut = tmp("fut", [CP, NB, TILES, CQ * D])
        fsum, past, flow, hidc, xT_b, yc, sq, sd, x1_b, rows = buffers(
            "c", ("fsum", CP, CQ * D), ("past", D, CH), ("flow", 2 * D, CH), ("hidc", H, CH), ("xTb", D, CH),
            ("yc", D, CH), ("sq", D, CH), ("sd", D, CH), ("x1b", D, CH), ("rows", CP, CQ * D))
        (c_s1, c_s2, c_sum, c_max, c_P, c_past, c_inv, c_flow, c_F, c_fT, c_H, c_hb, c_hc, c_O, c_yc, c_sq, c_V, c_sd,
         c_rs, c_x1, c_N, c_row) = [tsem(f"c_{i}") for i in range(22)]
        c_fut = [tsem(f"c_fut{b}") for b in range(NB)]
        c_xT = [tsem(f"c_xT{b}") for b in range(NB)]
        c_stT = [tsem(f"c_stT{b}") for b in range(NB)]
        c_st = [tsem(f"c_st{b}") for b in range(NB)]
        with nc.Block() as block:
            @block.sync
            def _(sp):
                def load_futures(c):
                    if c >= NB:
                        sp.wait_ge(c_sum, c - NB + 1)
                    for k in range(TILES):
                        sp.dma_start(fut[:, c % NB, k, :], future_c[k][c]).then_inc(c_fut[c % NB], 16)

                def load_x(c):
                    if c >= NB:
                        sp.wait_ge(c_O, c - NB + 1)
                    sp.dma_start(xT_b[:, c % NB, :], xT[c]).then_inc(c_xT[c % NB], 16)

                def store_T(c):
                    sp.wait_ge(c_x1, c + 1)
                    sp.dma_start(x1T[c], x1_b[:, c % NB, :]).then_inc(c_stT[c % NB], 16)

                def store_rows(c):
                    sp.wait_ge(c_row, c + 1)
                    sp.dma_start(x1_c[c], rows[:, c % NB, :]).then_inc(c_st[c % NB], 16)

                stages(load_futures, None, None, load_x, None, None, store_T, store_rows)
                all_stored(sp, c_stT)
                all_stored(sp, c_st)

            @block.gpsimd
            def _(pool):
                def sum_tables(c):
                    b = c % NB
                    pool.wait_ge(c_fut[b], 16 * TILES * (c // NB + 1))
                    if c >= NB:
                        pool.wait_ge(c_F, c - NB + 1)
                    pool.tensor_tensor(fsum[:, b, :], fut[:, b, 0, :], fut[:, b, 1, :], ALU.add).then_inc(c_s1, 1)
                    pool.wait_ge(c_s1, c + 1)
                    pool.tensor_tensor(fsum[:, b, :], fsum[:, b, :], fut[:, b, 2, :], ALU.add).then_inc(c_s2, 1)
                    pool.wait_ge(c_s2, c + 1)
                    pool.tensor_tensor(fsum[:, b, :], fsum[:, b, :], fut[:, b, 3, :], ALU.add).then_inc(c_sum, 1)

                stages(None, sum_tables)

            @block.vector
            def _(dve):
                def past_side(c):
                    b = c % NB
                    dve.wait_ge(c_P, c + 1)
                    dve.scalar_tensor_tensor(out=past[:, b, :], in0=chunk(cnt, c), scalar=b2pcol[:, 0:1],
                                             in1=bank[0][0:D, 0:CH], op0=ALU.mult, op1=ALU.add).then_inc(c_past, 1)
                    dve.tensor_scalar(chunk(cnt, c), chunk(cnt, c), 1.0, None, ALU.max).then_inc(c_max, 1)
                    dve.wait_ge(c_max, c + 1)
                    dve.reciprocal(chunk(cnt, c), chunk(cnt, c)).then_inc(c_inv, 1)
                    if c >= NB:
                        dve.wait_ge(c_H, c - NB + 1)
                    dve.wait_ge(c_past, c + 1)
                    dve.wait_ge(c_inv, c + 1)
                    dve.tensor_tensor(flow[0:D, b, :], past[:, b, :], chunk(cnt, c), ALU.mult).then_inc(c_flow, 1)

                def leaky(c):
                    b = c % NB
                    dve.wait_ge(c_hb, c + 1)
                    dve.scalar_tensor_tensor(out=hidc[:, b, :], in0=hidc[:, b, :], scalar=SLOPE, in1=hidc[:, b, :],
                                             op0=ALU.mult, op1=ALU.max).then_inc(c_hc, 1)

                def normal(c):
                    b = c % NB
                    dve.wait_ge(c_sd, c + 1)
                    dve.reciprocal(sd[:, b, :], sd[:, b, :]).then_inc(c_rs, 1)
                    if c >= NB:
                        dve.wait_ge(*stored(c_stT, c))
                        dve.wait_ge(c_N, c - NB + 1)
                    dve.wait_ge(c_rs, c + 1)
                    dve.tensor_tensor(x1_b[:, b, :], yc[:, b, :], sd[:, b, :], ALU.mult).then_inc(c_x1, 1)

                stages(None, past_side, None, leaky, None, normal)
                dve.wait_ge(c_P, CHUNKS)
                dve.memset(acc[0:D, :], 0.0)
                dve.tensor_copy(rel[:, :, :], rel0[:, :, :])
                dve.tensor_copy(base[:, :], base0[:, :])

            @block.scalar
            def _(act):
                def future_side(c):
                    if c >= NB:
                        act.wait_ge(c_H, c - NB + 1)
                    act.wait_ge(c_F, c + 1)
                    act.copy(natural(flow[D:2 * D, c % NB, :]), slots(bank[1][0:D, 0:CH])).then_inc(c_fT, 1)

                def hidden(c):
                    if c >= NB:
                        act.wait_ge(c_O, c - NB + 1)
                    act.wait_ge(c_H, c + 1)
                    act.activation(hidc[:, c % NB, :], bank[2][:, 0:CH], ACT.Identity, bias=bc1col[:, 0:1]).then_inc(c_hb, 1)

                def centred(c):
                    b = c % NB
                    if c >= NB:
                        act.wait_ge(c_x1, c - NB + 1)
                        act.wait_ge(c_V, c - NB + 1)
                    act.wait_ge(c_O, c + 1)
                    act.activation(sq[:, b, :], bank[3][0:D, 0:CH], ACT.Square, bias=bc2c[:, 0:1]).then_inc(c_sq, 1)
                    act.activation(yc[:, b, :], bank[3][0:D, 0:CH], ACT.Identity, bias=bc2c[:, 0:1]).then_inc(c_yc, 1)

                def deviation(c):
                    if c >= NB:
                        act.wait_ge(c_x1, c - NB + 1)
                    act.wait_ge(c_V, c + 1)
                    act.activation(sd[:, c % NB, :], bank[4][0:D, 0:CH], ACT.Sqrt, bias=eps[0:D, 0:1]).then_inc(c_sd, 1)

                def by_node(c):
                    if c >= NB:
                        act.wait_ge(*stored(c_st, c))
                    act.wait_ge(c_N, c + 1)
                    act.copy(rows[:, c % NB, :], bank[5][0:CP, 0:CQ * D]).then_inc(c_row, 1)

                stages(None, None, future_side, hidden, centred, deviation, by_node)

            @block.tensor
            def _(pe):
                def past_product(c):
                    if c >= 1:
                        pe.wait_ge(c_past, c)
                    pe.matmul(bank[0][0:D, 0:CH], w2p[:, :], chunk(acc, c), start=True, stop=True).then_inc(c_P, 1)

                def turn_futures(c):
                    pe.wait_ge(c_sum, c + 1)
                    if c >= 1:
                        pe.wait_ge(c_fT, c)
                    for q in range(CQ):
                        last = pe.transpose(bank[1][0:D, q * CP:(q + 1) * CP], fsum[:, c % NB, q * D:(q + 1) * D],
                                            ident[0:CP, 0:CP])
                    last.then_inc(c_F, 1)

                def hidden(c):
                    pe.wait_ge(c_flow, c + 1)
                    pe.wait_ge(c_fT, c + 1)
                    if c >= 1:
                        pe.wait_ge(c_hb, c)
                    pe.matmul(bank[2][:, 0:CH], wc1[:, :], flow[:, c % NB, :], start=True, stop=True).then_inc(c_H, 1)

                def centred(c):
                    b = c % NB
                    pe.wait_ge(c_xT[b], 16 * (c // NB + 1))
                    pe.wait_ge(c_hc, c + 1)
                    if c >= 1:
                        pe.wait_ge(c_yc, c)
                    pe.matmul(bank[3][0:D, 0:CH], wc2c[:, :], hidc[:, b, :], start=True, stop=False)
                    pe.matmul(bank[3][0:D, 0:CH], centre2[:, :], xT_b[:, b, :], start=False, stop=True).then_inc(c_O, 1)

                def variance(c):
                    pe.wait_ge(c_sq, c + 1)
                    if c >= 1:
                        pe.wait_ge(c_sd, c)
                    pe.matmul(bank[4][0:D, 0:CH], mean[:, :], sq[:, c % NB, :], start=True, stop=True).then_inc(c_V, 1)

                def by_node(c):
                    pe.wait_ge(c_x1, c + 1)
                    if c >= 1:
                        pe.wait_ge(c_row, c)
                    v = natural(x1_b[:, c % NB, :])
                    for q in range(CQ):
                        last = pe.transpose(bank[5][0:CP, q * D:(q + 1) * D], v[:, q, :], ident[0:D, 0:D])
                    last.then_inc(c_N, 1)

                stages(None, past_product, turn_futures, hidden, centred, variance, by_node)
        next_stage()

        for layer in range(2):
            oneh = tmp(f"oneh{layer}", [P, 2, TILES, W])
            gb1 = tmp(f"gb{layer}", [P, 2, TILES, D])
            frm = (x1, h1)[layer]
            frmT = (x1T, h1T)[layer]
            L = f"L{layer}_"
            edge_sems.clear()

            def lsem(name):
                return esem(L + name)

            t_prep = lsem("prep")
            t_gat = [sem(f"{L}gat{b}") for b in range(2)]
            t_gidx = lsem("gidx")
            t_open = lsem("open")
            t_oh = lsem("oh")
            t_S = lsem("S")
            t_acc = lsem("acc")
            with nc.Fori(0, rounds) as r:
                with nc.Block() as block:
                    @block.gpsimd
                    def _(pool):
                        def step(g, pair, b, early):
                            pool.wait_ge(t_gidx, g + 1)
                            if not early:
                                pool.wait_ge(t_S, g - 1)
                            pool.sem_inc(t_open, 1)
                            for q in range(TILES):
                                pool.indirect_dma_start(
                                    out=gb1[:, b, q, :], out_offset=None, in_=frm[:, :],
                                    in_offset=bass.IndirectOffsetOnAxis(ap=gidx[:, b, q:q + 1], axis=0)).then_inc(t_gat[b], 16)

                        over_groups(pool, step)

                    @block.vector
                    def _(dve):
                        windows(dve, t_prep)
                        dve.wait_ge(t_prep, 1)

                        def col(t, g):
                            return t[:, g, :] if isinstance(g, int) else t[:, bass.DynSlice(g, 1), :].rearrange("p a q -> p (a q)")

                        def add_sums(g, b):
                            at = dve.value_load(base_i[0:1, g:g + 1] if isinstance(g, int)
                                                else base_i[0:1, bass.DynSlice(g, 1)], min_val=0, max_val=N)
                            if not (isinstance(g, int) and g == 0):
                                dve.wait_ge(t_acc, g)
                            dve.wait_ge(t_S, g + 1)
                            v = acc[0:D, bass.DynSlice(at, W)]
                            dve.tensor_tensor(v, v, bank[b][0:D, 0:W], ALU.add).then_inc(t_acc, 1)

                        def step(g, pair, b, early):
                            if not early:
                                dve.wait_ge(t_S, g - 1)
                            dve.tensor_copy(gidx[:, b, :], col(src_i, g)).then_inc(t_gidx, 1)
                            dve.tensor_tensor(oneh[:, b, :, :], window_b,
                                              col(rel, g).unsqueeze(2).to_broadcast([P, TILES, W]),
                                              ALU.is_equal).then_inc(t_oh, 1)
                            if not (isinstance(g, int) and g == 0):
                                add_sums(g - 1, 1 - b)

                        over_groups(dve, step)
                        add_sums(GROUPS - 1, 0)
                        next_windows(dve)

                    @block.tensor
                    def _(pe):
                        def step(g, pair, b, early):
                            if not early:
                                pe.wait_ge(t_acc, g - 1)
                            pe.wait_ge(t_oh, g + 1)
                            pe.wait_ge(t_gat[b], r * gathered[b] + (64 * pair + 64))
                            pe.sem_inc(t_open, 1)
                            for q in range(TILES):
                                last = pe.matmul(bank[b][0:D, 0:W], gb1[:, b, q, :], oneh[:, b, q, :],
                                                 start=(q == 0), stop=(q == TILES - 1))
                            last.then_inc(t_S, 1)

                        over_groups(pe, step)

                clear(edge_sems)
            next_stage()

            kst, h_b, hsq, norm, h_out, rows = buffers(
                L, ("kst", 2 * D, CH), ("h", D, CH), ("hsq", D, CH), ("norm", D, CH), ("hout", D, CH), ("rows", CP, CQ * D))
            if layer == 1:
                res, y, yc, ysq, sd, last_b = buffers(L, ("res", D, CH), ("y", D, CH), ("yc", D, CH), ("ysq", D, CH),
                                                      ("sd", D, CH), ("last", D, CH))
            (u_k, u_H, u_h, u_hsq, u_V, u_n, u_max, u_inv, u_ho, u_N, u_row, u_y, u_m, u_yc, u_ysq, u_s, u_sd, u_rs,
             u_last) = [tsem(f"{L}u{i}") for i in range(19)]
            u_in = [tsem(f"{L}in{b}") for b in range(NB)]
            u_res = [tsem(f"{L}res{b}") for b in range(NB)]
            u_stT = [tsem(f"{L}stT{b}") for b in range(NB)]
            u_st = [tsem(f"{L}st{b}") for b in range(NB)]
            result = h_out if layer == 0 else last_b
            u_result = u_ho if layer == 0 else u_last
            with nc.Block() as block:
                @block.sync
                def _(sp):
                    def load_own(c):
                        if c >= NB:
                            sp.wait_ge(u_H, c - NB + 1)
                        sp.dma_start(kst[D:2 * D, c % NB, :], frmT[c]).then_inc(u_in[c % NB], 16)

                    def load_residual(c):
                        if c >= NB:
                            sp.wait_ge(u_y, c - NB + 1)
                        sp.dma_start(res[:, c % NB, :], x1T[c]).then_inc(u_res[c % NB], 16)

                    def store_T(c):
                        sp.wait_ge(u_ho, c + 1)
                        sp.dma_start(h1T[c], h_out[:, c % NB, :]).then_inc(u_stT[c % NB], 16)

                    def store_rows(c):
                        sp.wait_ge(u_row, c + 1)
                        sp.dma_start((h1_c, out_c)[layer][c], rows[:, c % NB, :]).then_inc(u_st[c % NB], 16)

                    if layer == 0:
                        stages(load_own, None, None, None, store_T, store_rows)
                        all_stored(sp, u_stT)
                    else:
                        stages(load_own, None, load_residual, None, None, None, None, store_rows)
                    all_stored(sp, u_st)

                @block.gpsimd
                def _(pool):
                    def mean_in(c):
                        if c >= NB:
                            pool.wait_ge(u_H, c - NB + 1)
                        pool.tensor_tensor(kst[0:D, c % NB, :], chunk(acc[0:D, :], c), chunk(cnt, c), ALU.mult).then_inc(u_k, 1)

                    def residual(c):
                        b = c % NB
                        if c >= NB:
                            pool.wait_ge(u_yc, c - NB + 1)
                        pool.wait_ge(u_res[b], 16 * (c // NB + 1))
                        pool.wait_ge(u_ho, c + 1)
                        pool.tensor_tensor(y[:, b, :], h_out[:, b, :], res[:, b, :], ALU.add).then_inc(u_y, 1)

                    stages(mean_in, None, None, residual if layer == 1 else None)

                @block.vector
                def _(dve):
                    def unit(c):
                        b = c % NB
                        dve.wait_ge(u_n, c + 1)
                        dve.tensor_scalar(norm[:, b, :], norm[:, b, :], EPS_NORM, None, ALU.max).then_inc(u_max, 1)
                        dve.wait_ge(u_max, c + 1)
                        dve.reciprocal(norm[:, b, :], norm[:, b, :]).then_inc(u_inv, 1)
                        if c >= NB and layer == 0:
                            dve.wait_ge(*stored(u_stT, c))
                            dve.wait_ge(u_N, c - NB + 1)
                        if c >= NB and layer == 1:
                            dve.wait_ge(u_y, c - NB + 1)
                        dve.wait_ge(u_h, c + 1)
                        dve.wait_ge(u_inv, c + 1)
                        dve.scalar_tensor_tensor(out=h_out[:, b, :], in0=h_b[:, b, :], scalar=0.0, in1=norm[:, b, :],
                                                 op0=ALU.max, op1=ALU.mult).then_inc(u_ho, 1)

                    def centre_y(c):
                        b = c % NB
                        if c >= NB:
                            dve.wait_ge(u_ysq, c - NB + 1)
                        dve.wait_ge(u_m, c + 1)
                        dve.tensor_tensor(yc[:, b, :], y[:, b, :], bank[3][0:D, 0:CH], ALU.subtract).then_inc(u_yc, 1)

                    def normal(c):
                        b = c % NB
                        dve.wait_ge(u_sd, c + 1)
                        dve.reciprocal(sd[:, b, :], sd[:, b, :]).then_inc(u_rs, 1)
                        if c >= NB:
                            dve.wait_ge(u_N, c - NB + 1)
                        dve.wait_ge(u_rs, c + 1)
                        dve.wait_ge(u_yc, c + 1)
                        dve.tensor_tensor(last_b[:, b, :], yc[:, b, :], sd[:, b, :], ALU.mult).then_inc(u_last, 1)

                    if layer == 0:
                        stages(None, None, unit)
                        dve.wait_ge(u_k, CHUNKS)
                        dve.memset(acc[0:D, :], 0.0)
                        dve.tensor_copy(rel[:, :, :], rel0[:, :, :])
                        dve.tensor_copy(base[:, :], base0[:, :])
                    else:
                        stages(None, None, unit, None, centre_y, normal)

                @block.scalar
                def _(act):
                    def hidden(c):
                        b = c % NB
                        if c >= NB:
                            act.wait_ge(u_ho, c - NB + 1)
                            act.wait_ge(u_V, c - NB + 1)
                        act.wait_ge(u_H, c + 1)
                        act.activation(hsq[:, b, :], bank[0][0:D, 0:CH], ACT.Square, bias=blcol[:, layer:layer + 1]).then_inc(u_hsq, 1)
                        act.activation(h_b[:, b, :], bank[0][0:D, 0:CH], ACT.Identity, bias=blcol[:, layer:layer + 1]).then_inc(u_h, 1)

                    def length(c):
                        if c >= NB:
                            act.wait_ge(u_ho, c - NB + 1)
                        act.wait_ge(u_V, c + 1)
                        act.activation(norm[:, c % NB, :], bank[1][0:D, 0:CH], ACT.Sqrt).then_inc(u_n, 1)

                    def square(c):
                        b = c % NB
                        if c >= NB:
                            act.wait_ge(u_s, c - NB + 1)
                        act.wait_ge(u_yc, c + 1)
                        act.activation(ysq[:, b, :], yc[:, b, :], ACT.Square).then_inc(u_ysq, 1)

                    def deviation(c):
                        if c >= NB:
                            act.wait_ge(u_last, c - NB + 1)
                        act.wait_ge(u_s, c + 1)
                        act.activation(sd[:, c % NB, :], bank[4][0:D, 0:CH], ACT.Sqrt, bias=eps[0:D, 0:1]).then_inc(u_sd, 1)

                    def by_node(c):
                        if c >= NB:
                            act.wait_ge(*stored(u_st, c))
                        act.wait_ge(u_N, c + 1)
                        act.copy(rows[:, c % NB, :], bank[2][0:CP, 0:CQ * D]).then_inc(u_row, 1)

                    if layer == 0:
                        stages(None, hidden, length, by_node)
                    else:
                        stages(None, hidden, length, None, square, deviation, by_node)

                @block.tensor
                def _(pe):
                    def hidden(c):
                        b = c % NB
                        pe.wait_ge(u_in[b], 16 * (c // NB + 1))
                        pe.wait_ge(u_k, c + 1)
                        if c >= 1:
                            pe.wait_ge(u_h, c)
                        pe.matmul(bank[0][0:D, 0:CH], wlrT[:, layer, :], kst[:, b, :], start=True, stop=True).then_inc(u_H, 1)

                    def length(c):
                        pe.wait_ge(u_hsq, c + 1)
                        if c >= 1:
                            pe.wait_ge(u_n, c)
                        pe.matmul(bank[1][0:D, 0:CH], ones[0:D, :], hsq[:, c % NB, :], start=True, stop=True).then_inc(u_V, 1)

                    def mean_y(c):
                        pe.wait_ge(u_y, c + 1)
                        if c >= 1:
                            pe.wait_ge(u_yc, c)
                        pe.matmul(bank[3][0:D, 0:CH], mean[:, :], y[:, c % NB, :], start=True, stop=True).then_inc(u_m, 1)

                    def variance(c):
                        pe.wait_ge(u_ysq, c + 1)
                        if c >= 1:
                            pe.wait_ge(u_sd, c)
                        pe.matmul(bank[4][0:D, 0:CH], mean[:, :], ysq[:, c % NB, :], start=True, stop=True).then_inc(u_s, 1)

                    def by_node(c):
                        pe.wait_ge(u_result, c + 1)
                        if c >= 1:
                            pe.wait_ge(u_row, c)
                        v = natural(result[:, c % NB, :])
                        for q in range(CQ):
                            last = pe.transpose(bank[2][0:CP, q * D:(q + 1) * D], v[:, q, :], ident[0:D, 0:D])
                        last.then_inc(u_N, 1)

                    if layer == 0:
                        stages(None, hidden, length, by_node)
                    else:
                        stages(None, hidden, length, None, mean_y, variance, by_node)
            next_stage()


_INS = ['x', 'src', 'dst', 'edge_attr_32', 'L0_gnn_W1f', 'L0_gnn_b1f', 'L0_gnn_W2f', 'L0_gnn_b2f',
        'L0_gnn_W1p', 'L0_gnn_b1p', 'L0_gnn_W2p', 'L0_gnn_b2p', 'L0_gnn_Wc1', 'L0_gnn_bc1', 'L0_gnn_Wc2', 'L0_gnn_bc2',
        'L1_gnn_Wl0', 'L1_gnn_bl0', 'L1_gnn_Wr0', 'L1_gnn_Wl1', 'L1_gnn_bl1', 'L1_gnn_Wr1']
_OUTS = [((N, D), 'float32')]


def kernel(**inputs):
    import numpy as _np
    import concourse.bacc as _bacc
    from concourse import mybir as _mybir
    from concourse.bass_utils import run_bass_kernel_spmd as _run

    nc = _bacc.Bacc("TRN2", target_bir_lowering=False, num_devices=1)
    arrays, args = {}, []
    for name in _INS:
        a = _np.ascontiguousarray(inputs[name])
        arrays[f"in_{name}_dram"] = a
        args.append(nc.dram_tensor(f"in_{name}_dram", a.shape, _mybir.dt.from_np(a.dtype), kind="ExternalInput").ap())
    for i, (shape, dtype) in enumerate(_OUTS):
        dt = _mybir.dt.from_np(_np.dtype(dtype))
        args.append(nc.dram_tensor(f"out_{i}_dram", shape, dt, kind="ExternalOutput").ap())
    build(nc, *args)
    r = _run(nc, [arrays], core_ids=[0])
    return r.results[0]["out_0_dram"]
```

```python
from contextlib import ExitStack

import concourse.bass as bass
from concourse import mybir

F32 = mybir.dt.float32
I32 = mybir.dt.int32
ALU = mybir.AluOpType
ACT = mybir.ActivationFunctionType
AX_X = mybir.AxisListType.X

P = 128
N = 12500
E = 200000
D = 64
DE = 32
H = 128
TILES = 4
GROUP = TILES * P
GROUPS = -(-E // GROUP)
LAST = E - GROUP
OVERLAP = (GROUPS - 1) * GROUP - LAST
PAIRS = (GROUPS - 1) // 2
W = 64
NW = N + W
CH = 500
CP, CQ = 125, 4
CHUNKS = N // CH
NB = 3
ROWS = 12800
PARTS = 4
ZCOLS = ROWS * D // P // PARTS
XPARTS = 5
XC = CHUNKS // XPARTS
HALF = NW // 2
XFIRST = 6
LOADS = [98, 98, 98, GROUPS - 3 * 98]
EPS_LN = 1e-5
EPS_NORM = 1e-12
SLOPE = 0.01


def build(nc, x, src, dst, ea, W1f, b1f, W2f, b2f, W1p, b1p, W2p, b2p, Wc1, bc1, Wc2, bc2,
          Wl0, bl0, Wr0, Wl1, bl1, Wr1, out):
    future = [nc.dram_tensor(f"future{q}", [ROWS, D], F32).ap() for q in range(TILES)]
    xT = nc.dram_tensor("xT", [D, NW], F32).ap()
    x1 = nc.dram_tensor("x1", [N, D], F32).ap()
    h1 = nc.dram_tensor("h1", [N, D], F32).ap()

    ctx = ExitStack()
    with ctx:
        def sb(name, shape, dt=F32):
            return ctx.enter_context(nc.sbuf_tensor(name, shape, dt))

        stage = [ExitStack()]

        def tmp(name, shape, dt=F32):
            return stage[0].enter_context(nc.sbuf_tensor(name, shape, dt))

        stage_sems = []

        def tsem(name):
            stage_sems.append(stage[0].enter_context(nc.semaphore(name)))
            return stage_sems[-1]

        def clear(sems):
            for s in sems:
                nc.sync.sem_clear(s)
            nc.all_engine_barrier()

        def next_stage():
            if stage_sems:
                clear(stage_sems)
            stage_sems.clear()
            stage[0].close()
            stage[0] = ExitStack()

        def ps(name, shape):
            return ctx.enter_context(nc.psum_tensor(name, shape, F32))

        def sem(name):
            return ctx.enter_context(nc.semaphore(name))

        bank = [ps(f"bank{i}", [P, 512]) for i in range(8)]

        acc = sb("acc", [P, NW])
        cnt = sb("cnt", [D, NW])

        ident = sb("ident", [P, P])
        mean = sb("mean", [D, D])
        triu = sb("triu", [P, P])
        ones = sb("ones", [P, D])
        window = sb("window", [P, W])
        window_i = sb("window_i", [P, W], I32)
        dump = sb("dump", [P, 1])
        dump_i = sb("dump_i", [P, 1], I32)
        eps = sb("eps", [P, 1])
        zero = sb("zero", [P, ZCOLS])

        w1px = sb("w1px", [D + 1, H])
        w1fx = sb("w1fx", [D, H])
        w1pe = sb("w1pe", [W + DE, H])
        w2f = sb("w2f", [H, D])
        w2p = sb("w2p", [H, D])
        b2frow = sb("b2frow", [P, D])
        b2pcol = sb("b2pcol", [D, 1])
        wc1 = sb("wc1", [2 * D, H])
        bc1col = sb("bc1col", [H, 1])
        wc2 = sb("wc2", [H, D])
        bc2col = sb("bc2col", [D, 1])
        wc2c = sb("wc2c", [H, D])
        xc = sb("xc", [D + 1, D])
        wlr = sb("wlr", [D, 2, 2 * D])
        wlrT = sb("wlrT", [2 * D, 2, D])
        blrow = sb("blrow", [CP, 2, D])
        inv = sb("inv", [CP, CHUNKS, CQ])

        src_i = sb("src_i", [P, GROUPS + 1, TILES], I32)
        rel0 = sb("rel0", [P, GROUPS, TILES])
        rel = sb("rel", [P, GROUPS, TILES])
        base0 = sb("base0", [1, GROUPS])
        base = sb("base", [1, GROUPS])
        base_i = sb("base_i", [1, GROUPS], I32)
        gidx = sb("gidx", [P, 2, TILES], I32)
        rounds_i = sb("rounds_i", [1, 1], I32)

        s_const = sem("s_const")
        s_weights = sem("s_weights")
        s_iota = sem("s_iota")

        def row(v):
            return v.rearrange("(a n) -> a n", a=1)

        def col1(v):
            return v.rearrange("(n a) -> n a", a=1)

        WEIGHTS = [
            (w1px[0:D, :], W1p[0:D, :]), (w1px[D:D + 1, :], row(b1p)), (w1fx[:, :], W1f[0:D, :]),
            (w1pe[W:W + DE, :], W1p[D:D + DE, :]), (w2f[:, :], W2f), (w2p[:, :], W2p),
            (b2frow[:, :], row(b2f).to_broadcast([P, D])), (b2pcol[:, :], col1(b2p)),
            (wc1[:, :], Wc1), (bc1col[:, :], col1(bc1)), (wc2[:, :], Wc2), (bc2col[:, :], col1(bc2)),
            (wlr[:, 0, 0:D], Wl0), (wlr[:, 0, D:2 * D], Wr0), (wlr[:, 1, 0:D], Wl1), (wlr[:, 1, D:2 * D], Wr1),
            (blrow[:, 0, :], row(bl0).to_broadcast([CP, D])), (blrow[:, 1, :], row(bl1).to_broadcast([CP, D])),
        ]

        def natural(t):
            return t.rearrange("k (p q) -> k q p", q=CQ)

        def slots(t):
            return t.rearrange("k (q p) -> k q p", q=CQ)

        src_g = tmp("src_g", [98, 4, GROUP], I32)
        dst_g = tmp("dst_g", [98, 4, GROUP], I32)
        src_f = src_g[:, :, :].bitcast(F32)
        dst_f = dst_g[:, :, :].bitcast(F32)
        low = tmp("low", [98, 4])
        high = tmp("high", [98, 4])
        span = tmp("span", [98, 4])
        spans = tmp("spans", [1, GROUPS])
        widest = tmp("widest", [1, 1])
        widest_i = tmp("widest_i", [1, 1], I32)
        more_i = tmp("more_i", [1, 1], I32)
        lastrows = LOADS[3]
        parts = [(0, 98, 0, 3), (0, lastrows, 3, 4)]
        x_all = acc[0:CP, 0:CHUNKS * CQ * D].rearrange("p (c k) -> p c k", c=CHUNKS)
        xT_all = cnt
        centre = tmp("centre", [D, D])
        wc2T = tmp("wc2T", [D, H])
        x_p = x.rearrange("(c p q) d -> p c (q d)", p=CP, q=CQ)

        (s_float, s_ext, s_rel, s_turn, s_turned, s_rowt, s_row, s_clear, s_centre, s_wt, s_wtc, s_wc,
         sA_zero, sA_t, sA_T) = [tsem(f"set{i}") for i in range(15)]
        sA_zeroed = sem("sA_zeroed")
        sA_pad = sem("sA_pad")
        s_idx = [tsem(f"s_idx{i}") for i in range(2)]
        sA_x = [tsem(f"sA_x{i}") for i in range(XPARTS)]
        sA_xT = [tsem(f"sA_xT{i}") for i in range(XPARTS)]
        with nc.Block() as block:
            @block.sync
            def _(sp):
                for i in range(XPARTS):
                    own = slice(i * XC, (i + 1) * XC)
                    sp.dma_start(x_all[:, own, :], x_p[:, own, :]).then_inc(sA_x[i], 16)
                for to, frm in WEIGHTS:
                    sp.dma_start(to, frm).then_inc(s_weights, 16)
                for i in range(XPARTS):
                    own = slice(i * XC * CH, (i + 1) * XC * CH)
                    sp.wait_ge(sA_T, (i + 1) * XC)
                    sp.dma_start(xT[:, own], xT_all[:, own]).then_inc(sA_xT[i], 16)

            @block.gpsimd
            def _(pool):
                nc.gpsimd.memset(ident[:, :], 0.0).then_inc(s_iota, 1)
                nc.gpsimd.memset(triu[:, :], 1.0).then_inc(s_iota, 1)
                nc.gpsimd.memset(ones[:, :], 1.0).then_inc(s_const, 1)
                nc.gpsimd.memset(mean[:, :], 1.0 / D).then_inc(s_const, 1)
                nc.gpsimd.memset(eps[:, :], EPS_LN).then_inc(s_const, 1)
                nc.gpsimd.iota(window_i[:, :], pattern=[[1, W]], base=0, channel_multiplier=0).then_inc(s_iota, 1)
                nc.gpsimd.iota(dump_i[:, :], pattern=[[0, 1]], base=N, channel_multiplier=1).then_inc(s_iota, 1)
                pool.wait_ge(s_iota, 4)
                nc.gpsimd.affine_select(out=ident[:, :], in_=ident[:, :], compare_op=ALU.not_equal, fill=1.0,
                                        base=0, pattern=[[-1, P]], channel_multiplier=1).then_inc(s_const, 1)
                nc.gpsimd.memset(zero[:, :], 0.0).then_inc(sA_zero, 1)
                nc.gpsimd.affine_select(out=triu[:, :], in_=triu[:, :], compare_op=ALU.is_ge, fill=0.0,
                                        base=0, pattern=[[1, P]], channel_multiplier=-1).then_inc(s_const, 1)
                nc.gpsimd.tensor_copy(window[:, :], window_i[:, :]).then_inc(s_const, 1)
                nc.gpsimd.tensor_copy(dump[:, :], dump_i[:, :]).then_inc(s_const, 1)

                def clear_table(q):
                    part = future[q].rearrange("(h p r) d -> h p (r d)", h=PARTS, p=P)
                    for h in range(PARTS):
                        pool.dma_start(part[h], zero[:, :]).then_inc(sA_zeroed, 16)

                pool.wait_ge(sA_zero, 1)
                pool.dma_start(xT[:, N:NW], zero[0:D, 0:W]).then_inc(sA_pad, 16)
                for i in range(XPARTS):
                    pool.wait_ge(sA_x[i], 16)
                for q in range(TILES // 2):
                    clear_table(q)
                pool.wait_ge(sA_T, (XPARTS - 1) * XC)
                for q in range(TILES // 2, TILES):
                    clear_table(q)
                pool.wait_ge(sA_t, CHUNKS)
                pool.memset(acc[:, 0:HALF], 0.0).then_inc(s_clear, 1)
                for i in range(XPARTS):
                    pool.wait_ge(sA_xT[i], 16)
                    pool.memset(cnt[:, i * XC * CH:(i + 1) * XC * CH], 0.0).then_inc(s_clear, 1)
                pool.memset(cnt[:, N:NW], 0.0).then_inc(s_clear, 1)
                pool.wait_ge(sA_pad, 16)

            @block.scalar
            def _(act):
                for k, (a, to) in enumerate(((dst, dst_g), (src, src_g))):
                    g0 = 0
                    for c, size in enumerate(LOADS):
                        full = size - (c == 3)
                        act.dma_start(to[0:full, c, :], a[g0 * GROUP:(g0 + full) * GROUP].rearrange(
                            "(g e) -> g e", e=GROUP)).then_inc(s_idx[k], 16)
                        g0 += size
                    act.dma_start(to[lastrows - 1:lastrows, 3, :],
                                  a[LAST:E].rearrange("(g e) -> g e", e=GROUP)).then_inc(s_idx[k], 16)
                for c in range(CHUNKS):
                    act.wait_ge(sA_t, c + 1)
                    act.copy(natural(xT_all[:, c * CH:(c + 1) * CH]), slots(bank[c % 2][0:D, 0:CH])).then_inc(sA_T, 1)

            @block.tensor
            def _(pe):
                def turn_x(c):
                    pe.wait_ge(sA_x[c // XC], 16)
                    if c >= 2:
                        pe.wait_ge(sA_T, c - 1)
                    for q in range(CQ):
                        last = pe.transpose(bank[c % 2][0:D, q * CP:(q + 1) * CP],
                                            x_all[:, c, q * D:(q + 1) * D], ident[0:CP, 0:CP])
                    last.then_inc(sA_t, 1)

                def turn_indices(k, frm, c):
                    size = LOADS[c]
                    if k >= 2:
                        pe.wait_ge(s_turned, k - 1)
                    v = frm[0:size, c, :].rearrange("g (p q) -> g q p", q=TILES)
                    for q in range(TILES):
                        last = pe.transpose(bank[2 + k % 2][:, q * size:(q + 1) * size], v[:, q, :],
                                            ident[0:size, 0:size])
                    last.then_inc(s_turn, 1)

                pe.wait_ge(s_const, 7)
                for c in range(XFIRST):
                    turn_x(c)
                pe.wait_ge(s_rel, 6)
                pe.wait_ge(s_float, 4)
                for k in range(8):
                    turn_indices(k, (dst_f, src_f)[k % 2], k // 2)
                    turn_x(XFIRST + k)
                g0 = 0
                for c, size in enumerate(LOADS):
                    pe.transpose(bank[4][0:1, g0:g0 + size], low[0:size, c:c + 1], ident[0:size, 0:size])
                    last = pe.transpose(bank[5][0:1, g0:g0 + size], span[0:size, c:c + 1], ident[0:size, 0:size])
                    g0 += size
                last.then_inc(s_rowt, 1)
                for c in range(XFIRST + 8, CHUNKS):
                    turn_x(c)
                pe.wait_ge(s_weights, 16 * len(WEIGHTS))
                for k in range(4):
                    pe.transpose(bank[6][0:D, k * D:(k + 1) * D], wlr[:, k // 2, (k % 2) * D:(k % 2 + 1) * D],
                                 ident[0:D, 0:D])
                pe.transpose(bank[6][0:D, 2 * H:3 * H], wc2[:, :], ident[:, :]).then_inc(s_wt, 1)
                pe.wait_ge(s_wtc, 1)
                pe.wait_ge(s_centre, 1)
                pe.matmul(bank[7][:, 0:D], wc2T[:, :], centre[:, :], start=True, stop=True)
                pe.matmul(bank[7][0:1, D:2 * D], bc2col[:, :], centre[:, :], start=True, stop=True).then_inc(s_wc, 1)

            @block.vector
            def _(dve):
                dve.wait_ge(s_idx[0], 16 * 5)
                for p0, p1, c0, c1 in parts:
                    dve.tensor_copy(dst_f[p0:p1, c0:c1, :], dst_g[p0:p1, c0:c1, :]).then_inc(s_float, 1)
                dve.wait_ge(s_float, 2)
                for p0, p1, c0, c1 in parts:
                    dve.tensor_reduce(low[p0:p1, c0:c1], dst_f[p0:p1, c0:c1, :], AX_X, ALU.min).then_inc(s_ext, 1)
                    dve.tensor_reduce(high[p0:p1, c0:c1], dst_f[p0:p1, c0:c1, :], AX_X, ALU.max).then_inc(s_ext, 1)
                dve.wait_ge(s_ext, 4)
                for c in range(4):
                    dve.tensor_scalar(dst_f[0:LOADS[c], c, :], dst_f[0:LOADS[c], c, :], low[0:LOADS[c], c:c + 1],
                                      None, ALU.subtract).then_inc(s_rel, 1)
                for p0, p1, c0, c1 in parts:
                    dve.tensor_tensor(span[p0:p1, c0:c1], high[p0:p1, c0:c1], low[p0:p1, c0:c1],
                                      ALU.subtract).then_inc(s_rel, 1)
                dve.wait_ge(s_idx[1], 16 * 5)
                for p0, p1, c0, c1 in parts:
                    dve.tensor_copy(src_f[p0:p1, c0:c1, :], src_g[p0:p1, c0:c1, :]).then_inc(s_float, 1)
                dve.wait_ge(s_float, 4)
                dve.wait_ge(s_const, 7)
                dve.tensor_tensor(centre[:, :], ident[0:D, 0:D], mean[:, :], ALU.subtract).then_inc(s_centre, 1)
                dve.wait_ge(s_centre, 1)
                dve.tensor_scalar(xc[0:D, :], centre[:, :], 2.0, None, ALU.mult)
                k = 0
                g0 = 0
                for c, size in enumerate(LOADS):
                    for to in (rel0, src_i):
                        dve.wait_ge(s_turn, k + 1)
                        t = bank[2 + k % 2][:, 0:TILES * size].rearrange("p (q g) -> p q g", q=TILES)
                        dve.tensor_copy(to[:, g0:g0 + size, :].rearrange("p g q -> p q g"), t).then_inc(s_turned, 1)
                        k += 1
                    g0 += size
                dve.wait_ge(s_turned, 8)
                dve.memset(src_i[:, GROUPS, :], 0)
                dve.memset(rel0[0:OVERLAP // TILES, GROUPS - 1, :], -1.0e6).then_inc(s_turned, 1)
                dve.wait_ge(s_rowt, 1)
                dve.tensor_copy(base0[:, :], bank[4][0:1, 0:GROUPS]).then_inc(s_turned, 1)
                dve.tensor_copy(spans[:, :], bank[5][0:1, 0:GROUPS]).then_inc(s_row, 1)
                dve.wait_ge(s_row, 1)
                dve.tensor_reduce(widest[:, :], spans[:, :], AX_X, ALU.max).then_inc(s_row, 1)
                dve.wait_ge(s_row, 2)
                dve.tensor_copy(widest_i[:, :], widest[:, :]).then_inc(s_row, 1)
                dve.wait_ge(s_row, 3)
                dve.tensor_single_scalar(more_i[:, :], widest_i[:, :], W.bit_length() - 1, ALU.logical_shift_right).then_inc(s_row, 1)
                dve.wait_ge(s_row, 4)
                dve.tensor_scalar(rounds_i[:, :], more_i[:, :], 1, None, ALU.add).then_inc(s_row, 1)
                dve.wait_ge(s_turned, 10)
                dve.tensor_copy(rel[:, :, :], rel0[:, :, :])
                dve.tensor_copy(base[:, :], base0[:, :])
                dve.wait_ge(s_wt, 1)
                dve.tensor_copy(wc2T[:, :], bank[6][0:D, 2 * H:3 * H]).then_inc(s_wtc, 1)
                turned = bank[6][0:D, 0:4 * D].rearrange("p (l a d) -> p l a d", l=2, a=2)
                dve.tensor_copy(wlrT[0:D, :, :], turned[:, :, 0, :])
                dve.tensor_copy(wlrT[D:2 * D, :, :], turned[:, :, 1, :])
                dve.wait_ge(s_wc, 1)
                dve.tensor_copy(wc2c[:, :], bank[7][:, 0:D])
                dve.tensor_copy(xc[D:D + 1, :], bank[7][0:1, D:2 * D])
                dve.wait_ge(sA_t, CHUNKS)
                dve.memset(acc[:, HALF:NW], 0.0)

        next_stage()

        rounds = nc.values_load(rounds_i[0:1, 0:1], min_val=1, max_val=N // W + 1)

        srcm = tmp("srcm", [P, GROUPS, TILES])
        inwin = tmp("inwin", [P, GROUPS, TILES])
        comb = tmp("comb", [P, 2, TILES, W + DE])
        xwin = tmp("xwin", [D, 2, W])
        wwin = tmp("wwin", [W + DE + 1, 2, H])
        gbuf = tmp("gbuf", [P, 2, TILES, D])
        srcT = tmp("srcT", [D + 1, 2, GROUP])
        skey = tmp("skey", [P, 2, TILES])
        equal = tmp("equal", [P, 2, TILES, P])
        later = tmp("later", [P, 2, TILES])
        away = tmp("away", [P, 2, TILES])
        pick = tmp("pick", [P, 2, TILES])
        sidx = tmp("sidx", [P, 2, TILES], I32)
        featT = tmp("featT", [W + DE + 1, 2, GROUP])
        hidf = tmp("hidf", [H, 2, GROUP])
        msg = tmp("msg", [P, 2, TILES, D])
        sbuf = tmp("sbuf", [P, 2, TILES, D])
        hidp = tmp("hidp", [P, 2, GROUP])

        psR, psT, psF, psP, psM, psD, psS, psX = bank
        psW = psD[0:W, TILES * D:TILES * D + H]

        edge_sems = []

        def esem(name):
            edge_sems.append(stage[0].enter_context(nc.semaphore(name)))
            return edge_sems[-1]

        s_prep = esem("s_prep")
        s_wedge = esem("s_wedge")
        s_ea = [esem(f"s_ea{b}") for b in range(2)]
        s_win = [esem(f"s_win{b}") for b in range(2)]
        s_gat = [sem(f"s_gat{b}") for b in range(2)]
        s_sc = [sem(f"s_sc{q}") for q in range(TILES)]
        gathered = [16 * TILES * (PAIRS + 1), 16 * TILES * PAIRS]
        added = 16 * GROUPS
        s_open = esem("s_open")
        s_scdone = esem("s_scdone")
        s_pe_open = esem("s_pe_open")
        s_sp_open = esem("s_sp_open")
        s_gidx = esem("s_gidx")
        s_sm = esem("s_sm")
        s_oh = esem("s_oh")
        s_eu = esem("s_eu")
        s_away = esem("s_away")
        s_pick = esem("s_pick")
        s_sidx = esem("s_sidx")
        s_msb = esem("s_msb")
        s_ones = esem("s_ones")
        s_W = esem("s_W")
        s_wwin = esem("s_wwin")
        s_X = esem("s_X")
        s_srcT = esem("s_srcT")
        s_pslope = esem("s_pslope")
        s_acc = esem("s_acc")
        s_stk = esem("s_stk")
        s_slope = esem("s_slope")
        s_hf = esem("s_hf")
        s_hp = esem("s_hp")
        s_sb = esem("s_sb")
        s_R = esem("s_R")
        s_T = esem("s_T")
        s_F = esem("s_F")
        s_P = esem("s_P")
        s_M = esem("s_M")
        s_D = esem("s_D")
        s_S = esem("s_S")

        def over_groups(eng, step, first=0):
            step(0, 0, 0, True)
            step(1, 0, 1, True)
            with eng.Fori(1, PAIRS) as i:
                step(2 * i, i, 0, False)
                step(2 * i + 1, i, 1, False)
            step(GROUPS - 1, PAIRS, 0, False)

        def final(g):
            return isinstance(g, int) and g == GROUPS - 1

        def windows(dve, done):
            dve.tensor_scalar(base_i[:, :], base[:, :], float(N), None, ALU.min).then_inc(done, 1)

        def next_windows(dve):
            dve.tensor_scalar(rel[:, :, :], rel[:, :, :], -float(W), None, ALU.add)
            dve.tensor_scalar(base[:, :], base[:, :], float(W), None, ALU.add)

        ea_main = ea[0:(GROUPS - 1) * GROUP, :].rearrange("(g p q) f -> g p q f", p=P, q=TILES)
        ea_last = ea[LAST:E, :].rearrange("(p q) f -> p q f", q=TILES)
        window_b = window[:, :].unsqueeze(1).to_broadcast([P, TILES, W])

        with nc.Fori(0, rounds) as r:
            with nc.Block() as block:
                @block.sync
                def _(sp):
                    for b in range(2):
                        sp.dma_start(wwin[W:W + DE, b, :], W1f[D:D + DE, :]).then_inc(s_wedge, 16)
                        sp.dma_start(wwin[W + DE:W + DE + 1, b, :], row(b1f)).then_inc(s_wedge, 16)
                    sp.wait_ge(s_prep, 4)

                    def step(g, pair, b, early):
                        if not early:
                            sp.wait_ge(s_T, g - 1)
                        sp.dma_start(comb[:, b, :, W:W + DE], ea_last if final(g) else ea_main[g]).then_inc(s_ea[b], 16)
                        at = sp.value_load(base_i[0:1, g:g + 1] if isinstance(g, int)
                                            else base_i[0:1, bass.DynSlice(g, 1)], min_val=0, max_val=N)
                        if not early:
                            sp.wait_ge(s_W, g - 1)
                        sp.sem_inc(s_sp_open, 1)
                        sp.dma_start(xwin[:, b, :], xT[:, bass.DynSlice(at, W)]).then_inc(s_win[b], 16)

                    over_groups(sp, step)

                @block.gpsimd
                def _(pool):
                    def gathers(b):
                        for q in range(TILES):
                            pool.indirect_dma_start(
                                out=gbuf[:, b, q, :], out_offset=None, in_=x[:, :],
                                in_offset=bass.IndirectOffsetOnAxis(ap=gidx[:, b, q:q + 1], axis=0)).then_inc(s_gat[b], 16)

                    def scatters(g, b):
                        if isinstance(g, int) and g == 0:
                            pool.wait_ge(sA_zeroed, 16 * PARTS * TILES)
                        if not (isinstance(g, int) and g == 0):
                            for q in range(TILES):
                                pool.wait_ge(s_sc[q], r * added + 16 * g)
                        pool.wait_ge(s_sidx, g + 1)
                        pool.wait_ge(s_sb, g + 1)
                        pool.sem_inc(s_scdone, 1)
                        for q in range(TILES):
                            pool.indirect_dma_start(
                                out=future[q][:, :],
                                out_offset=bass.IndirectOffsetOnAxis(ap=sidx[:, b, q:q + 1], axis=0),
                                in_=sbuf[:, b, q, :], in_offset=None, compute_op=ALU.add).then_inc(s_sc[q], 16)

                    pool.wait_ge(s_gidx, 1)
                    gathers(0)
                    pool.memset(featT[W + DE:W + DE + 1, :, :], 1.0).then_inc(s_ones, 1)
                    pool.memset(srcT[D:D + 1, :, :], 1.0).then_inc(s_ones, 1)

                    def step(g, pair, b, early):
                        if not final(g):
                            if not (isinstance(g, int) and g == 0):
                                pool.wait_ge(s_X, g)
                            pool.wait_ge(s_gidx, g + 2)
                            pool.sem_inc(s_open, 1)
                            gathers(1 - b)
                        if not (isinstance(g, int) and g == 0):
                            scatters(g - 1, 1 - b)

                    over_groups(pool, step)
                    scatters(GROUPS - 1, 0)
                    for q in range(TILES):
                        pool.wait_ge(s_sc[q], r * added + added)

                @block.vector
                def _(dve):
                    for b in range(2):
                        dve.tensor_copy(gidx[:, b, :], src_i[:, b, :]).then_inc(s_gidx, 1)
                    windows(dve, s_prep)
                    dve.tensor_single_scalar(inwin[:, :, :], rel[:, :, :], 0.0, ALU.is_ge).then_inc(s_prep, 1)
                    dve.tensor_scalar(srcm[:, :, :], src_i[:, 0:GROUPS, :], dump[:, 0:1], None, ALU.subtract).then_inc(s_prep, 1)
                    dve.wait_ge(s_prep, 3)
                    dve.scalar_tensor_tensor(out=inwin[:, :, :], in0=rel[:, :, :], scalar=float(W), in1=inwin[:, :, :],
                                             op0=ALU.is_lt, op1=ALU.mult).then_inc(s_prep, 1)
                    dve.wait_ge(s_prep, 4)
                    dve.tensor_tensor(srcm[:, :, :], srcm[:, :, :], inwin[:, :, :], ALU.mult).then_inc(s_prep, 1)
                    dve.wait_ge(s_prep, 5)
                    dve.tensor_scalar(srcm[:, :, :], srcm[:, :, :], dump[:, 0:1], None, ALU.add).then_inc(s_prep, 1)
                    dve.wait_ge(s_prep, 6)

                    def col(t, g):
                        return t[:, g, :] if isinstance(g, int) else t[:, bass.DynSlice(g, 1), :].rearrange("p a q -> p (a q)")

                    def add_sums(g):
                        at = dve.value_load(base_i[0:1, g:g + 1] if isinstance(g, int)
                                            else base_i[0:1, bass.DynSlice(g, 1)], min_val=0, max_val=N)
                        if not (isinstance(g, int) and g == 0):
                            dve.wait_ge(s_acc, 2 * g)
                        dve.wait_ge(s_S, g + 1)
                        v = acc[:, bass.DynSlice(at, W)]
                        dve.tensor_tensor(v, v, psS[:, 0:W], ALU.add).then_inc(s_acc, 1)
                        v = cnt[:, bass.DynSlice(at, W)]
                        dve.tensor_tensor(v, v, psS[0:D, W:2 * W], ALU.add).then_inc(s_acc, 1)

                    def messages(g, b):
                        dve.wait_ge(s_M, g + 1)
                        dve.tensor_tensor(msg[:, b, :, :], psM[:, 0:TILES * D].rearrange("p (q d) -> p q d", q=TILES),
                                          b2frow[:, :].unsqueeze(1).to_broadcast([P, TILES, D]),
                                          ALU.add).then_inc(s_msb, 1)
                        dve.wait_ge(s_away, g + 1)
                        dve.wait_ge(s_eu, 4 * g + 4)
                        dve.scalar_tensor_tensor(out=pick[:, b, :], in0=later[:, b, :], scalar=1.0, in1=away[:, b, :],
                                                 op0=ALU.is_equal, op1=ALU.mult).then_inc(s_pick, 1)
                        if not (isinstance(g, int) and g < 2):
                            dve.wait_ge(s_scdone, g)
                        dve.wait_ge(s_pick, g + 1)
                        dve.tensor_scalar(sidx[:, b, :], pick[:, b, :], dump[:, 0:1], None, ALU.add).then_inc(s_sidx, 1)

                    def front(g, b):
                        dve.tensor_copy(skey[:, b, :], col(srcm, g)).then_inc(s_sm, 1)
                        dve.tensor_tensor(comb[:, b, :, 0:W], window_b,
                                          col(rel, g).unsqueeze(2).to_broadcast([P, TILES, W]),
                                          ALU.is_equal).then_inc(s_oh, 1)
                        dve.wait_ge(s_sm, g + 1)
                        dve.tensor_scalar(away[:, b, :], skey[:, b, :], dump[:, 0:1], None, ALU.subtract).then_inc(s_away, 1)

                    front(0, 0)

                    def step(g, pair, b, early):
                        if not (isinstance(g, int) and g == 0):
                            messages(g - 1, 1 - b)
                        if not early:
                            dve.wait_ge(s_D, g - 1)
                        dve.wait_ge(s_R, g + 1)
                        for q in range(TILES):
                            dve.scalar_tensor_tensor(out=equal[:, b, q, :], in0=psR[:, q * P:(q + 1) * P],
                                                     scalar=skey[:, b, q:q + 1], in1=triu[:, :],
                                                     op0=ALU.is_equal, op1=ALU.mult,
                                                     accum_out=later[:, b, q:q + 1]).then_inc(s_eu, 1)
                        if not (isinstance(g, int) and g == 0):
                            add_sums(g - 1)
                        if not final(g):
                            dve.wait_ge(s_X, g + 1)
                            dve.tensor_copy(gidx[:, b, :], col(src_i, g + 2)).then_inc(s_gidx, 1)
                            front(g + 1, 1 - b)
                        dve.wait_ge(s_slope, g + 1)
                        dve.tensor_tensor(hidf[:, b, :], hidf[:, b, :], psF[:, :], ALU.max).then_inc(s_hf, 1)
                        dve.wait_ge(s_pslope, g + 1)
                        dve.tensor_tensor(hidp[:, b, :], hidp[:, b, :], psP[:, :], ALU.max).then_inc(s_hp, 1)

                    over_groups(dve, step)
                    messages(GROUPS - 1, 0)
                    add_sums(GROUPS - 1)
                    next_windows(dve)

                @block.scalar
                def _(act):
                    def summed(g, b):
                        if not (isinstance(g, int) and g < 2):
                            act.wait_ge(s_scdone, g)
                        act.wait_ge(s_D, g + 1)
                        act.copy(sbuf[:, b, :, :], psD[:, 0:TILES * D].rearrange("p (q d) -> p q d", q=TILES)).then_inc(s_sb, 1)

                    def step(g, pair, b, early):
                        if not early:
                            act.wait_ge(s_P, g - 1)
                        act.wait_ge(s_T, g + 1)
                        act.copy(featT[0:W + DE, b, :], psT[0:W + DE, :]).then_inc(s_stk, 1)
                        act.wait_ge(s_W, g + 1)
                        act.copy(wwin[0:W, b, :], psW).then_inc(s_wwin, 1)
                        act.wait_ge(s_X, g + 1)
                        act.copy(srcT[0:D, b, :], psX[0:D, :]).then_inc(s_srcT, 1)
                        if not (isinstance(g, int) and g == 0):
                            summed(g - 1, 1 - b)
                        if not early:
                            act.wait_ge(s_M, g - 1)
                        act.wait_ge(s_F, g + 1)
                        act.activation(hidf[:, b, :], psF[:, :], ACT.Copy, scale=SLOPE).then_inc(s_slope, 1)
                        if not early:
                            act.wait_ge(s_S, g - 1)
                        act.wait_ge(s_P, g + 1)
                        act.activation(hidp[:, b, :], psP[:, :], ACT.Copy, scale=SLOPE).then_inc(s_pslope, 1)
                    over_groups(act, step)
                    summed(GROUPS - 1, 0)

                @block.tensor
                def _(pe):
                    def sums(g, b):
                        if not (isinstance(g, int) and g == 0):
                            pe.wait_ge(s_acc, 2 * g)
                        pe.wait_ge(s_hp, g + 1)
                        for q in range(TILES):
                            pe.matmul(psS[:, 0:W], hidp[:, b, q * P:(q + 1) * P], comb[:, b, q, 0:W],
                                      start=(q == 0), stop=(q == TILES - 1))
                        for q in range(TILES):
                            last = pe.matmul(psS[0:D, W:2 * W], ones[:, :], comb[:, b, q, 0:W],
                                             start=(q == 0), stop=(q == TILES - 1))
                        last.then_inc(s_S, 1)

                    def messages(g, b):
                        if not (isinstance(g, int) and g == 0):
                            pe.wait_ge(s_msb, g)
                        pe.wait_ge(s_hf, g + 1)
                        for q in range(TILES):
                            last = pe.matmul(psM[:, q * D:(q + 1) * D], hidf[:, b, q * P:(q + 1) * P], w2f[:, :],
                                             start=True, stop=True)
                        last.then_inc(s_M, 1)

                    def equal_sums(g, b):
                        if not (isinstance(g, int) and g == 0):
                            pe.wait_ge(s_sb, g)
                        if not final(g):
                            pe.wait_ge(s_wwin, g + 2)
                        pe.wait_ge(s_eu, 4 * g + 4)
                        pe.wait_ge(s_msb, g + 1)
                        for q in range(TILES):
                            last = pe.matmul(psD[:, q * D:(q + 1) * D], equal[:, b, q, :], msg[:, b, q, :],
                                             start=True, stop=True)
                        last.then_inc(s_D, 1)

                    pe.wait_ge(s_wedge, 64)
                    pe.wait_ge(s_ones, 2)

                    def step(g, pair, b, early):
                        first = isinstance(g, int) and g == 0
                        if not first:
                            pe.wait_ge(s_eu, 4 * g)
                        pe.wait_ge(s_sm, g + 1)
                        for q in range(TILES):
                            last = pe.transpose(psR[:, q * P:(q + 1) * P],
                                                skey[:, b, q:q + 1].to_broadcast([P, P]), ident[:, :])
                        last.then_inc(s_R, 1)
                        pe.wait_ge(s_ea[b], 16 * pair + 16)
                        if not first:
                            pe.wait_ge(s_stk, g)
                        pe.wait_ge(s_oh, g + 1)
                        for q in range(TILES):
                            last = pe.transpose(psT[0:W + DE, q * P:(q + 1) * P], comb[:, b, q, :], ident[:, :])
                        last.then_inc(s_T, 1)
                        if not first:
                            messages(g - 1, 1 - b)
                        pe.wait_ge(s_win[b], 16 * pair + 16)
                        if not first:
                            pe.wait_ge(s_wwin, g)
                        if not early:
                            pe.wait_ge(s_sb, g - 1)
                        pe.sem_inc(s_pe_open, 1)
                        pe.matmul(psW, xwin[:, b, :], w1fx[:, :], start=True, stop=True).then_inc(s_W, 1)
                        pe.wait_ge(s_gat[b], r * gathered[b] + (64 * pair + 64))
                        if not first:
                            pe.wait_ge(s_srcT, g)
                        pe.sem_inc(s_pe_open, 1)
                        for q in range(TILES):
                            last = pe.transpose(psX[0:D, q * P:(q + 1) * P], gbuf[:, b, q, :], ident[:, :])
                        last.then_inc(s_X, 1)
                        if not first:
                            sums(g - 1, 1 - b)
                            equal_sums(g - 1, 1 - b)
                        if not first:
                            pe.wait_ge(s_hf, g)
                        pe.wait_ge(s_wwin, g + 1)
                        pe.wait_ge(s_stk, g + 1)
                        pe.matmul(psF[:, :], wwin[:, b, :], featT[:, b, :], start=True, stop=True).then_inc(s_F, 1)
                        if not first:
                            pe.wait_ge(s_hp, g)
                        pe.wait_ge(s_srcT, g + 1)
                        for q in range(TILES):
                            tile = slice(q * P, (q + 1) * P)
                            pe.matmul(psP[:, tile], featT[W:W + DE, b, tile], w1pe[W:W + DE, :], start=True, stop=False)
                            last = pe.matmul(psP[:, tile], srcT[:, b, tile], w1px[:, :], start=False, stop=True)
                        last.then_inc(s_P, 1)
                    over_groups(pe, step)
                    messages(GROUPS - 1, 0)
                    sums(GROUPS - 1, 0)
                    equal_sums(GROUPS - 1, 0)

            clear(edge_sems)

        next_stage()

        def stages(*works):
            for t in range(CHUNKS + len(works) - 1):
                for s in reversed(range(len(works))):
                    if works[s] and 0 <= t - s < CHUNKS:
                        works[s](t - s)

        def buffers(where, *shapes):
            return [tmp(f"{where}_{name}", [rows, NB, n]) for name, rows, n in shapes]

        x1_c = x1.rearrange("(c p q) d -> c p (q d)", p=CP, q=CQ)
        h1_c = h1.rearrange("(c p q) d -> c p (q d)", p=CP, q=CQ)
        out_c = out.rearrange("(c p q) d -> c p (q d)", p=CP, q=CQ)
        future_c = [f[0:N, :].rearrange("(c p q) d -> c p (q d)", p=CP, q=CQ) for f in future]

        def chunk(t, c):
            return t[:, c * CH:(c + 1) * CH]

        def stored(sems, c, each=1):
            return sems[c % NB], 16 * each * (c // NB)

        def all_stored(eng, sems, each=1):
            for b in range(NB):
                eng.wait_ge(sems[b], 16 * each * len(range(b, CHUNKS, NB)))

        def by_slot(t):
            return t.rearrange("p (q d) -> p q d", q=CQ)

        def per_node(t):
            return t.unsqueeze(2).to_broadcast([CP, CQ, D])

        fut = tmp("fut", [CP, NB, TILES, CQ * D])
        fsum, past, flow, hidc, xT_b, yc, sq, var, rows = buffers(
            "c", ("fsum", CP, CQ * D), ("past", D, CH), ("flow", 2 * D, CH), ("hidc", H, CH), ("xTb", D + 1, CH),
            ("yc", CP, CQ * D), ("sq", CP, CQ * D), ("var", CP, CQ), ("rows", CP, CQ * D))
        (c_ones, c_s1, c_s2, c_sum, c_P, c_C, c_past, c_max, c_inv, c_I, c_flow, c_F, c_fT, c_H, c_hb, c_hc, c_O, c_yc,
         c_sq, c_var, c_sd, c_rs, c_rows, c_T, c_x1T, c_spread) = [tsem(f"c_{i}") for i in range(26)]
        c_fut = [tsem(f"c_fut{b}") for b in range(NB)]
        c_xT = [tsem(f"c_xT{b}") for b in range(NB)]
        c_st = [tsem(f"c_st{b}") for b in range(NB)]
        psP, psFu, psH, psO, psTr, psC = bank[0:6]
        psI = bank[6:8]
        with nc.Block() as block:
            @block.sync
            def _(sp):
                def load_futures(c):
                    if c >= NB:
                        sp.wait_ge(c_sum, c - NB + 1)
                    for k in range(TILES):
                        sp.dma_start(fut[:, c % NB, k, :], future_c[k][c]).then_inc(c_fut[c % NB], 16)

                def load_x(c):
                    if c >= NB:
                        sp.wait_ge(c_O, c - NB + 1)
                    sp.dma_start(xT_b[0:D, c % NB, :], xT[:, c * CH:(c + 1) * CH]).then_inc(c_xT[c % NB], 16)

                def store_rows(c):
                    sp.wait_ge(c_rows, c + 1)
                    sp.dma_start(x1_c[c], rows[:, c % NB, :]).then_inc(c_st[c % NB], 16)

                stages(load_futures, None, load_x, None, None, None, None, store_rows)
                all_stored(sp, c_st)

            @block.gpsimd
            def _(pool):
                def sum_tables(c):
                    b = c % NB
                    pool.wait_ge(c_fut[b], 16 * TILES * (c // NB + 1))
                    if c >= NB:
                        pool.wait_ge(c_F, c - NB + 1)
                    pool.tensor_tensor(fsum[:, b, :], fut[:, b, 0, :], fut[:, b, 1, :], ALU.add).then_inc(c_s1, 1)
                    pool.wait_ge(c_s1, c + 1)
                    pool.tensor_tensor(fsum[:, b, :], fsum[:, b, :], fut[:, b, 2, :], ALU.add).then_inc(c_s2, 1)
                    pool.wait_ge(c_s2, c + 1)
                    pool.tensor_tensor(fsum[:, b, :], fsum[:, b, :], fut[:, b, 3, :], ALU.add).then_inc(c_sum, 1)

                def clear_sums(c):
                    pool.wait_ge(c_P, c + 1)
                    pool.memset(chunk(acc[0:D, :], c), 0.0)

                pool.memset(acc[0:D, N:NW], 0.0)
                pool.tensor_copy(rel[:, :, :], rel0[:, :, :])
                pool.tensor_copy(base[:, :], base0[:, :])
                stages(None, sum_tables, None, clear_sums)

            @block.vector
            def _(dve):
                dve.memset(xT_b[D:D + 1, :, :], 1.0).then_inc(c_ones, 1)

                def past_side(c):
                    b = c % NB
                    if c >= NB:
                        dve.wait_ge(c_flow, c - NB + 1)
                    dve.wait_ge(c_P, c + 1)
                    dve.scalar_tensor_tensor(out=past[:, b, :], in0=chunk(cnt, c), scalar=b2pcol[:, 0:1],
                                             in1=psP[0:D, 0:CH], op0=ALU.mult, op1=ALU.add).then_inc(c_past, 1)
                    dve.wait_ge(c_C, c + 1)
                    dve.tensor_scalar(inv[:, c, :], psC[0:CP, 0:CQ], 1.0, None, ALU.max).then_inc(c_max, 1)
                    dve.wait_ge(c_max, c + 1)
                    dve.reciprocal(inv[:, c, :], inv[:, c, :]).then_inc(c_inv, 1)

                def past_mean(c):
                    b = c % NB
                    if c >= NB:
                        dve.wait_ge(c_H, c - NB + 1)
                    dve.wait_ge(c_past, c + 1)
                    dve.wait_ge(c_I, c + 1)
                    dve.tensor_tensor(natural(flow[0:D, b, :]), natural(past[:, b, :]), slots(psI[c % 2][0:D, 0:CH]),
                                      ALU.mult).then_inc(c_flow, 1)

                def leaky(c):
                    b = c % NB
                    dve.wait_ge(c_hb, c + 1)
                    dve.scalar_tensor_tensor(out=hidc[:, b, :], in0=hidc[:, b, :], scalar=SLOPE, in1=hidc[:, b, :],
                                             op0=ALU.mult, op1=ALU.max).then_inc(c_hc, 1)

                def variance(c):
                    b = c % NB
                    if c >= NB:
                        dve.wait_ge(c_rs, c - NB + 1)
                    dve.wait_ge(c_sq, c + 1)
                    dve.tensor_reduce(var[:, b, :], by_slot(sq[:, b, :]), AX_X, ALU.add).then_inc(c_var, 1)

                def normal(c):
                    b = c % NB
                    dve.wait_ge(c_sd, c + 1)
                    dve.reciprocal(var[:, b, :], var[:, b, :]).then_inc(c_rs, 1)
                    if c >= NB:
                        dve.wait_ge(*stored(c_st, c))
                        dve.wait_ge(c_T, c - NB + 1)
                    dve.wait_ge(c_rs, c + 1)
                    dve.tensor_tensor(by_slot(rows[:, b, :]), by_slot(yc[:, b, :]), per_node(var[:, b, :]),
                                      ALU.mult).then_inc(c_rows, 1)

                stages(None, past_side, past_mean, leaky, None, variance, normal)

            @block.scalar
            def _(act):
                def future_side(c):
                    if c >= NB:
                        act.wait_ge(c_H, c - NB + 1)
                    act.wait_ge(c_F, c + 1)
                    act.copy(natural(flow[D:2 * D, c % NB, :]), slots(psFu[0:D, 0:CH])).then_inc(c_fT, 1)

                def hidden(c):
                    if c >= NB:
                        act.wait_ge(c_O, c - NB + 1)
                    act.wait_ge(c_H, c + 1)
                    act.activation(hidc[:, c % NB, :], psH[:, 0:CH], ACT.Identity, bias=bc1col[:, 0:1]).then_inc(c_hb, 1)

                def centred(c):
                    b = c % NB
                    if c >= NB:
                        act.wait_ge(c_rows, c - NB + 1)
                        act.wait_ge(c_var, c - NB + 1)
                    act.wait_ge(c_O, c + 1)
                    act.activation(sq[:, b, :], psO[0:CP, 0:CQ * D], ACT.Square).then_inc(c_sq, 1)
                    act.copy(yc[:, b, :], psO[0:CP, 0:CQ * D]).then_inc(c_yc, 1)

                def deviation(c):
                    b = c % NB
                    act.wait_ge(c_var, c + 1)
                    act.activation(var[:, b, :], var[:, b, :], ACT.Sqrt, bias=eps[0:CP, 0:1], scale=1.0 / D).then_inc(c_sd, 1)

                def turned(c):
                    act.wait_ge(c_T, c + 1)
                    act.copy(natural(chunk(acc[D:2 * D, :], c)), slots(psTr[0:D, 0:CH])).then_inc(c_x1T, 1)

                def keep_inverse(c):
                    act.wait_ge(c_past, c + 1)
                    act.wait_ge(c_C, c + 1)
                    act.wait_ge(c_I, c + 1)
                    act.wait_ge(c_flow, c + 1)
                    act.copy(natural(chunk(cnt, c)), slots(psI[c % 2][0:D, 0:CH])).then_inc(c_spread, 1)

                def spread(c):
                    hidden(c)
                    keep_inverse(c)

                stages(None, None, future_side, spread, centred, deviation, None, turned)

            @block.tensor
            def _(pe):
                pe.wait_ge(c_ones, 1)

                def past_side(c):
                    if c >= 1:
                        pe.wait_ge(c_past, c)
                    pe.matmul(psP[0:D, 0:CH], w2p[:, :], chunk(acc, c), start=True, stop=True).then_inc(c_P, 1)
                    if c >= 1:
                        pe.wait_ge(c_max, c)
                    v = natural(chunk(cnt[0:1, :], c))
                    for q in range(CQ):
                        last = pe.transpose(psC[0:CP, q:q + 1], v[:, q, :], ident[0:1, 0:1])
                    last.then_inc(c_C, 1)

                def spread_inverse(c):
                    pe.wait_ge(c_inv, c + 1)
                    if c >= 2:
                        pe.wait_ge(c_spread, c - 1)
                    for q in range(CQ):
                        last = pe.transpose(psI[c % 2][0:D, q * CP:(q + 1) * CP], inv[:, c, q:q + 1].to_broadcast([CP, D]),
                                            ident[0:CP, 0:CP])
                    last.then_inc(c_I, 1)
                    pe.wait_ge(c_sum, c + 1)
                    if c >= 1:
                        pe.wait_ge(c_fT, c)
                    for q in range(CQ):
                        last = pe.transpose(psFu[0:D, q * CP:(q + 1) * CP], fsum[:, c % NB, q * D:(q + 1) * D],
                                            ident[0:CP, 0:CP])
                    last.then_inc(c_F, 1)

                def hidden(c):
                    pe.wait_ge(c_flow, c + 1)
                    pe.wait_ge(c_fT, c + 1)
                    if c >= 1:
                        pe.wait_ge(c_hb, c)
                    pe.matmul(psH[:, 0:CH], wc1[:, :], flow[:, c % NB, :], start=True, stop=True).then_inc(c_H, 1)

                def centred(c):
                    b = c % NB
                    pe.wait_ge(c_xT[b], 16 * (c // NB + 1))
                    pe.wait_ge(c_hc, c + 1)
                    if c >= 1:
                        pe.wait_ge(c_yc, c)
                    for q in range(CQ):
                        o = psO[0:CP, q * D:(q + 1) * D]
                        pe.matmul(o, natural(hidc[:, b, :])[:, q, :], wc2c[:, :], start=True, stop=False)
                        last = pe.matmul(o, natural(xT_b[:, b, :])[:, q, :], xc[:, :], start=False, stop=True)
                    last.then_inc(c_O, 1)

                def turn_back(c):
                    pe.wait_ge(c_rows, c + 1)
                    if c >= 1:
                        pe.wait_ge(c_x1T, c)
                    for q in range(CQ):
                        last = pe.transpose(psTr[0:D, q * CP:(q + 1) * CP], rows[:, c % NB, q * D:(q + 1) * D],
                                            ident[0:CP, 0:CP])
                    last.then_inc(c_T, 1)

                stages(None, past_side, spread_inverse, hidden, centred, None, None, turn_back)
        next_stage()

        for layer in range(2):
            oneh = tmp(f"oneh{layer}", [P, 2, TILES, W])
            gb1 = tmp(f"gb{layer}", [P, 2, TILES, D])
            frm = (x1, h1)[layer]
            L = f"L{layer}_"
            edge_sems.clear()

            def lsem(name):
                return esem(L + name)

            t_prep = lsem("prep")
            t_gat = [sem(f"{L}gat{b}") for b in range(2)]
            t_gidx = lsem("gidx")
            t_open = lsem("open")
            t_oh = lsem("oh")
            t_S = lsem("S")
            t_acc = lsem("acc")
            with nc.Fori(0, rounds) as r:
                with nc.Block() as block:
                    @block.gpsimd
                    def _(pool):
                        def step(g, pair, b, early):
                            pool.wait_ge(t_gidx, g + 1)
                            if not early:
                                pool.wait_ge(t_S, g - 1)
                            pool.sem_inc(t_open, 1)
                            for q in range(TILES):
                                pool.indirect_dma_start(
                                    out=gb1[:, b, q, :], out_offset=None, in_=frm[:, :],
                                    in_offset=bass.IndirectOffsetOnAxis(ap=gidx[:, b, q:q + 1], axis=0)).then_inc(t_gat[b], 16)

                        over_groups(pool, step)

                    @block.vector
                    def _(dve):
                        windows(dve, t_prep)
                        dve.wait_ge(t_prep, 1)

                        def col(t, g):
                            return t[:, g, :] if isinstance(g, int) else t[:, bass.DynSlice(g, 1), :].rearrange("p a q -> p (a q)")

                        def add_sums(g, b):
                            at = dve.value_load(base_i[0:1, g:g + 1] if isinstance(g, int)
                                                else base_i[0:1, bass.DynSlice(g, 1)], min_val=0, max_val=N)
                            if not (isinstance(g, int) and g == 0):
                                dve.wait_ge(t_acc, g)
                            dve.wait_ge(t_S, g + 1)
                            v = acc[0:D, bass.DynSlice(at, W)]
                            dve.tensor_tensor(v, v, bank[b][0:D, 0:W], ALU.add).then_inc(t_acc, 1)

                        def step(g, pair, b, early):
                            if not early:
                                dve.wait_ge(t_S, g - 1)
                            dve.tensor_copy(gidx[:, b, :], col(src_i, g)).then_inc(t_gidx, 1)
                            dve.tensor_tensor(oneh[:, b, :, :], window_b,
                                              col(rel, g).unsqueeze(2).to_broadcast([P, TILES, W]),
                                              ALU.is_equal).then_inc(t_oh, 1)
                            if not (isinstance(g, int) and g == 0):
                                add_sums(g - 1, 1 - b)

                        over_groups(dve, step)
                        add_sums(GROUPS - 1, 0)
                        next_windows(dve)

                    @block.tensor
                    def _(pe):
                        def step(g, pair, b, early):
                            if not early:
                                pe.wait_ge(t_acc, g - 1)
                            pe.wait_ge(t_oh, g + 1)
                            pe.wait_ge(t_gat[b], r * gathered[b] + (64 * pair + 64))
                            pe.sem_inc(t_open, 1)
                            for q in range(TILES):
                                last = pe.matmul(bank[b][0:D, 0:W], gb1[:, b, q, :], oneh[:, b, q, :],
                                                 start=(q == 0), stop=(q == TILES - 1))
                            last.then_inc(t_S, 1)

                        over_groups(pe, step)

                clear(edge_sems)
            next_stage()

            h_b, hsq, norm, rows = buffers(
                L, ("h", CP, CQ * D), ("hsq", CP, CQ * D), ("norm", CP, CQ), ("rows", CP, CQ * D))
            if layer == 1:
                res, y, yc, ysq, tot, var, last_b = buffers(
                    L, ("res", CP, CQ * D), ("y", CP, CQ * D), ("yc", CP, CQ * D), ("ysq", CP, CQ * D), ("tot", CP, CQ),
                    ("var", CP, CQ), ("last", CP, CQ * D))
            (u_scaled, u_A, u_h, u_hsq, u_n, u_max, u_inv, u_rows, u_T, u_hT, u_y, u_tot, u_mean, u_yc,
             u_ysq, u_sd, u_rs, u_last) = [tsem(f"{L}u{i}") for i in range(18)]
            u_res = [tsem(f"{L}res{b}") for b in range(NB)]
            u_st = [tsem(f"{L}st{b}") for b in range(NB)]
            psA = bank[0:2]
            psTr = bank[2:4]
            with nc.Block() as block:
                @block.sync
                def _(sp):
                    def load_residual(c):
                        if c >= NB:
                            sp.wait_ge(u_y, c - NB + 1)
                        sp.dma_start(res[:, c % NB, :], x1_c[c]).then_inc(u_res[c % NB], 16)

                    def store_h(c):
                        sp.wait_ge(u_rows, c + 1)
                        sp.dma_start(h1_c[c], rows[:, c % NB, :]).then_inc(u_st[c % NB], 16)

                    def store_out(c):
                        sp.wait_ge(u_last, c + 1)
                        sp.dma_start(out_c[c], last_b[:, c % NB, :]).then_inc(u_st[c % NB], 16)

                    if layer == 0:
                        stages(None, None, None, None, store_h)
                    else:
                        stages(None, load_residual, None, None, None, None, None, None, store_out)
                    all_stored(sp, u_st)

                if layer == 0:
                    @block.gpsimd
                    def _(pool):
                        def scale(c):
                            v = chunk(acc[0:D, :], c)
                            pool.tensor_tensor(v, v, chunk(cnt, c), ALU.mult).then_inc(u_scaled, 1)

                        def clear_sums(c):
                            pool.wait_ge(u_A, c + 1)
                            pool.memset(chunk(acc[0:D, :], c), 0.0)

                        pool.memset(acc[0:D, N:NW], 0.0)
                        pool.tensor_copy(rel[:, :, :], rel0[:, :, :])
                        pool.tensor_copy(base[:, :], base0[:, :])
                        stages(scale, None, clear_sums)

                if layer == 1:
                    @block.gpsimd
                    def _(pool):
                        def scale(c):
                            v = chunk(acc[0:D, :], c)
                            pool.tensor_tensor(v, v, chunk(cnt, c), ALU.mult).then_inc(u_scaled, 1)

                        def residual(c):
                            b = c % NB
                            if c >= NB:
                                pool.wait_ge(u_yc, c - NB + 1)
                            pool.wait_ge(u_res[b], 16 * (c // NB + 1))
                            pool.wait_ge(u_rows, c + 1)
                            pool.tensor_tensor(y[:, b, :], rows[:, b, :], res[:, b, :], ALU.add).then_inc(u_y, 1)

                        def centre_y(c):
                            b = c % NB
                            if c >= NB:
                                pool.wait_ge(u_ysq, CQ * (c - NB + 1))
                                pool.wait_ge(u_last, c - NB + 1)
                            pool.wait_ge(u_mean, c + 1)
                            pool.tensor_tensor(by_slot(yc[:, b, :]), by_slot(y[:, b, :]), per_node(tot[:, b, :]),
                                               ALU.subtract).then_inc(u_yc, 1)

                        stages(scale, None, None, None, residual, centre_y)

                @block.vector
                def _(dve):
                    def combine(c):
                        b = c % NB
                        if c >= NB:
                            dve.wait_ge(u_hsq, CQ * (c - NB + 1))
                        dve.wait_ge(u_A, c + 1)
                        dve.tensor_tensor(by_slot(h_b[:, b, :]), by_slot(psA[c % 2][0:CP, 0:CQ * D]),
                                          blrow[:, layer, :].unsqueeze(1).to_broadcast([CP, CQ, D]),
                                          ALU.add).then_inc(u_h, 1)

                    def unit(c):
                        b = c % NB
                        dve.wait_ge(u_n, c + 1)
                        dve.tensor_scalar(norm[:, b, :], norm[:, b, :], EPS_NORM, None, ALU.max).then_inc(u_max, 1)
                        dve.wait_ge(u_max, c + 1)
                        dve.reciprocal(norm[:, b, :], norm[:, b, :]).then_inc(u_inv, 1)
                        if c >= NB and layer == 0:
                            dve.wait_ge(*stored(u_st, c))
                            dve.wait_ge(u_T, c - NB + 1)
                        if c >= NB and layer == 1:
                            dve.wait_ge(u_y, c - NB + 1)
                        dve.wait_ge(u_inv, c + 1)
                        dve.scalar_tensor_tensor(out=by_slot(rows[:, b, :]), in0=by_slot(h_b[:, b, :]), scalar=0.0,
                                                 in1=per_node(norm[:, b, :]), op0=ALU.max, op1=ALU.mult).then_inc(u_rows, 1)

                    def mean_y(c):
                        b = c % NB
                        if c >= NB:
                            dve.wait_ge(u_yc, c - NB + 1)
                        dve.wait_ge(u_y, c + 1)
                        dve.tensor_reduce(tot[:, b, :], by_slot(y[:, b, :]), AX_X, ALU.add).then_inc(u_tot, 1)
                        dve.wait_ge(u_tot, c + 1)
                        dve.tensor_scalar(tot[:, b, :], tot[:, b, :], 1.0 / D, None, ALU.mult).then_inc(u_mean, 1)

                    def normal(c):
                        b = c % NB
                        dve.wait_ge(u_sd, c + 1)
                        dve.reciprocal(var[:, b, :], var[:, b, :]).then_inc(u_rs, 1)
                        if c >= NB:
                            dve.wait_ge(*stored(u_st, c))
                        dve.wait_ge(u_yc, c + 1)
                        dve.wait_ge(u_rs, c + 1)
                        dve.tensor_tensor(by_slot(last_b[:, b, :]), by_slot(yc[:, b, :]), per_node(var[:, b, :]),
                                          ALU.mult).then_inc(u_last, 1)

                    if layer == 0:
                        stages(None, None, combine, unit)
                    else:
                        stages(None, None, combine, unit, None, mean_y, None, normal)

                @block.scalar
                def _(act):
                    def length(c):
                        b = c % NB
                        if c >= NB:
                            act.wait_ge(u_rows, c - NB + 1)
                        act.wait_ge(u_h, c + 1)
                        for q in range(CQ):
                            act.activation(hsq[:, b, q * D:(q + 1) * D], h_b[:, b, q * D:(q + 1) * D], ACT.Square,
                                           accum_out=norm[:, b, q:q + 1]).then_inc(u_hsq, 1)
                        act.wait_ge(u_hsq, CQ * (c + 1))
                        act.activation(norm[:, b, :], norm[:, b, :], ACT.Sqrt).then_inc(u_n, 1)

                    def turned(c):
                        act.wait_ge(u_T, c + 1)
                        act.copy(natural(chunk(acc[D:2 * D, :], c)), slots(psTr[c % 2][0:D, 0:CH])).then_inc(u_hT, 1)

                    def deviation(c):
                        b = c % NB
                        if c >= NB:
                            act.wait_ge(u_last, c - NB + 1)
                        act.wait_ge(u_yc, c + 1)
                        for q in range(CQ):
                            act.activation(ysq[:, b, q * D:(q + 1) * D], yc[:, b, q * D:(q + 1) * D], ACT.Square,
                                           accum_out=var[:, b, q:q + 1]).then_inc(u_ysq, 1)
                        act.wait_ge(u_ysq, CQ * (c + 1))
                        act.activation(var[:, b, :], var[:, b, :], ACT.Sqrt, bias=eps[0:CP, 0:1], scale=1.0 / D).then_inc(u_sd, 1)

                    if layer == 0:
                        stages(None, None, length, None, turned)
                    else:
                        stages(None, None, length, None, None, None, deviation)

                @block.tensor
                def _(pe):
                    def products(c):
                        pe.wait_ge(u_scaled, c + 1)
                        if c >= 2:
                            pe.wait_ge(u_h, c - 1)
                        v = natural(chunk(acc, c))
                        for q in range(CQ):
                            last = pe.matmul(psA[c % 2][0:CP, q * D:(q + 1) * D], v[:, q, :], wlrT[:, layer, :],
                                             start=True, stop=True)
                        last.then_inc(u_A, 1)

                    def turn_back(c):
                        pe.wait_ge(u_rows, c + 1)
                        if c >= 2:
                            pe.wait_ge(u_hT, c - 1)
                        for q in range(CQ):
                            last = pe.transpose(psTr[c % 2][0:D, q * CP:(q + 1) * CP], rows[:, c % NB, q * D:(q + 1) * D],
                                                ident[0:CP, 0:CP])
                        last.then_inc(u_T, 1)

                    if layer == 0:
                        stages(None, products, None, None, turn_back)
                    else:
                        stages(None, products)
            next_stage()


_INS = ['x', 'src', 'dst', 'edge_attr_32', 'L0_gnn_W1f', 'L0_gnn_b1f', 'L0_gnn_W2f', 'L0_gnn_b2f',
        'L0_gnn_W1p', 'L0_gnn_b1p', 'L0_gnn_W2p', 'L0_gnn_b2p', 'L0_gnn_Wc1', 'L0_gnn_bc1', 'L0_gnn_Wc2', 'L0_gnn_bc2',
        'L1_gnn_Wl0', 'L1_gnn_bl0', 'L1_gnn_Wr0', 'L1_gnn_Wl1', 'L1_gnn_bl1', 'L1_gnn_Wr1']
_OUTS = [((N, D), 'float32')]


def kernel(**inputs):
    import numpy as _np
    import concourse.bacc as _bacc
    from concourse import mybir as _mybir
    from concourse.bass_utils import run_bass_kernel_spmd as _run

    nc = _bacc.Bacc("TRN2", target_bir_lowering=False, num_devices=1)
    arrays, args = {}, []
    for name in _INS:
        a = _np.ascontiguousarray(inputs[name])
        arrays[f"in_{name}_dram"] = a
        args.append(nc.dram_tensor(f"in_{name}_dram", a.shape, _mybir.dt.from_np(a.dtype), kind="ExternalInput").ap())
    for i, (shape, dtype) in enumerate(_OUTS):
        dt = _mybir.dt.from_np(_np.dtype(dtype))
        args.append(nc.dram_tensor(f"out_{i}_dram", shape, dt, kind="ExternalOutput").ap())
    build(nc, *args)
    r = _run(nc, [arrays], core_ids=[0])
    return r.results[0]["out_0_dram"]
```
